# Optimizing a Trainium2 kernel written in Bass

```python
import numpy as np
import jax
import jax.numpy as jnp

def _softmax(x, axis=-1):
    return jax.nn.softmax(x, axis=axis)
def _gelu(x):
    return jax.nn.gelu(x, approximate=True)
def _silu(x):
    return jax.nn.silu(x)
def _sigmoid(x):
    return jax.nn.sigmoid(x)
def _layernorm(x, axis=-1, eps=1e-5):
    m = jnp.mean(x, axis=axis, keepdims=True)
    v = jnp.var(x, axis=axis, keepdims=True)
    return (x - m) / jnp.sqrt(v + eps)
def _scatter_add(tgt, idx, src, axis=0):
    return tgt.at[idx].add(src)
def _segment_sum(src, seg, n):
    return jax.ops.segment_sum(src, seg, n)

kernel_name = 'mk_adj_resnorm_d2_adj_512_904aca'

def setup_inputs(seed: int = 0):
    np.random.seed(seed)
    _w = jnp.asarray
    def _rec_inputs():
        import jax
        import jax.numpy as jnp
        _gk = jax.random.key(seed)
        x = -0.0002928 + 1 * jax.random.normal(jax.random.fold_in(_gk, 1), (128, 128, 512), jnp.float32)
        _a = jax.random.bernoulli(jax.random.fold_in(_gk, 2), 0.0625, (128, 128))
        _a = jnp.logical_or(_a, jnp.swapaxes(_a, -1, -2))
        _a = jnp.logical_or(_a, jnp.eye(128, dtype=bool))
        _af = _a.astype(jnp.float32)
        adj = _af
        return x, adj
    x, adj = _rec_inputs()
    def _L0_gnn_setup():
        import jax, jax.numpy as jnp
        import numpy as np
        B, N, D, H = (4, 2048, 512, 8)
        HD = D // H
        key = jax.random.key(seed)
        ks = jax.random.split(key, 10)
        x = jax.random.normal(ks[0], (B, N, D), dtype=jnp.float32)
        adj = (jax.random.uniform(ks[1], (N, N)) < 0.1).astype(jnp.float32)
        s = 1.0 / np.sqrt(D)
        Wq = jax.random.normal(ks[2], (D, D), dtype=jnp.float32) * s
        Wk = jax.random.normal(ks[3], (D, D), dtype=jnp.float32) * s
        Wv = jax.random.normal(ks[4], (D, D), dtype=jnp.float32) * s
        Wo = jax.random.normal(ks[5], (D, D), dtype=jnp.float32) * s
        bq = jnp.zeros((D,), jnp.float32)
        bk = jnp.zeros((D,), jnp.float32)
        bv = jnp.zeros((D,), jnp.float32)
        bo = jnp.zeros((D,), jnp.float32)
        return {'x': x, 'adj': adj, 'Wq': Wq, 'bq': bq, 'Wk': Wk, 'bk': bk, 'Wv': Wv, 'bv': bv, 'Wo': Wo, 'bo': bo}
    _L0_gnn_all = _L0_gnn_setup()
    _L0_gnn_in = {k: v for k, v in _L0_gnn_all.items() if k in ('Wq', 'bq', 'Wk', 'bk', 'Wv', 'bv', 'Wo', 'bo', )}
    del _L0_gnn_all

    def _L1_gnn_setup():
        import jax, jax.numpy as jnp
        import numpy as np
        B, N, D = (4, 2048, 512)
        H, HD = (8, 64)
        key = jax.random.key(seed)
        ks = jax.random.split(key, 6)
        x = jax.random.normal(ks[0], (B, N, D), dtype=jnp.float32)
        adj = (jax.random.uniform(ks[1], (N, N)) < 0.1).astype(jnp.float32)
        adj = jnp.maximum(adj, jnp.eye(N, dtype=jnp.float32))
        s = 0.02
        Wq = jax.random.normal(ks[2], (D, H * HD), dtype=jnp.float32) * s
        Wk = jax.random.normal(ks[3], (D, H * HD), dtype=jnp.float32) * s
        Wv = jax.random.normal(ks[4], (D, H * HD), dtype=jnp.float32) * s
        bq = jnp.zeros((H * HD,), dtype=jnp.float32)
        bk = jnp.zeros((H * HD,), dtype=jnp.float32)
        bv = jnp.zeros((H * HD,), dtype=jnp.float32)
        return {'x': x, 'adj': adj, 'Wq': Wq, 'bq': bq, 'Wk': Wk, 'bk': bk, 'Wv': Wv, 'bv': bv}
    _L1_gnn_all = _L1_gnn_setup()
    _L1_gnn_in = {k: v for k, v in _L1_gnn_all.items() if k in ('Wq', 'bq', 'Wk', 'bk', 'Wv', 'bv', )}
    del _L1_gnn_all

    return {
        "x": x,
        "adj": adj,
        "L0_gnn_Wq": _L0_gnn_in["Wq"],
        "L0_gnn_bq": _L0_gnn_in["bq"],
        "L0_gnn_Wk": _L0_gnn_in["Wk"],
        "L0_gnn_bk": _L0_gnn_in["bk"],
        "L0_gnn_Wv": _L0_gnn_in["Wv"],
        "L0_gnn_bv": _L0_gnn_in["bv"],
        "L0_gnn_Wo": _L0_gnn_in["Wo"],
        "L0_gnn_bo": _L0_gnn_in["bo"],
        "L1_gnn_Wq": _L1_gnn_in["Wq"],
        "L1_gnn_bq": _L1_gnn_in["bq"],
        "L1_gnn_Wk": _L1_gnn_in["Wk"],
        "L1_gnn_bk": _L1_gnn_in["bk"],
        "L1_gnn_Wv": _L1_gnn_in["Wv"],
        "L1_gnn_bv": _L1_gnn_in["bv"],
    }

def reference(x, adj, L0_gnn_Wq, L0_gnn_bq, L0_gnn_Wk, L0_gnn_bk, L0_gnn_Wv, L0_gnn_bv, L0_gnn_Wo, L0_gnn_bo, L1_gnn_Wq, L1_gnn_bq, L1_gnn_Wk, L1_gnn_bk, L1_gnn_Wv, L1_gnn_bv):
    import jax
    import jax.numpy as jnp
    def _L0_gnn_ref(x, adj, Wq, bq, Wk, bk, Wv, bv, Wo, bo):
        import jax, jax.numpy as jnp
        import numpy as np
        B, N, D, H = (4, 2048, 512, 8)
        HD = D // H
        b, n, d = x.shape
        q = (x @ Wq + bq).reshape(b, n, H, HD)
        k = (x @ Wk + bk).reshape(b, n, H, HD)
        v = (x @ Wv + bv).reshape(b, n, H, HD)
        scores = jnp.einsum('bqhd,bkhd->bhqk', q, k) / jnp.sqrt(jnp.float32(HD))
        scores = scores + (1.0 - adj)[None, None, :, :] * -1000000000.0
        attn = jax.nn.softmax(scores, axis=-1)
        out = jnp.einsum('bhqk,bkhd->bqhd', attn, v).reshape(b, n, d)
        return out @ Wo + bo

    def _L1_gnn_ref(x, adj, Wq, bq, Wk, bk, Wv, bv):
        import jax, jax.numpy as jnp
        import numpy as np
        B, N, D = (4, 2048, 512)
        H, HD = (8, 64)
        b, n, _ = x.shape
        q = (x @ Wq + bq).reshape(b, n, H, HD)
        k = (x @ Wk + bk).reshape(b, n, H, HD)
        v = (x @ Wv + bv).reshape(b, n, H, HD)
        scores = jnp.einsum('bihd,bjhd->bhij', q, k) / jnp.sqrt(jnp.float32(HD))
        mask = jnp.where(adj == 0, jnp.float32(-1000000000.0), jnp.float32(0.0))
        scores = scores + mask[None, None, :, :]
        weights = jax.nn.softmax(scores, axis=-1)
        out = jnp.einsum('bhij,bjhd->bihd', weights, v)
        return out.reshape(b, n, H * HD)

    x = _layernorm(x + _L0_gnn_ref(x, adj, L0_gnn_Wq, L0_gnn_bq, L0_gnn_Wk, L0_gnn_bk, L0_gnn_Wv, L0_gnn_bv, L0_gnn_Wo, L0_gnn_bo), axis=-1)
    x = _layernorm(x + _L1_gnn_ref(x, adj, L1_gnn_Wq, L1_gnn_bq, L1_gnn_Wk, L1_gnn_bk, L1_gnn_Wv, L1_gnn_bv), axis=-1)
    return x


_drawn_inputs = setup_inputs


def setup_inputs(seed=0):
    import zlib

    import numpy as np

    out = dict(_drawn_inputs(seed))
    spreads = {'L0_gnn_bq': (0.0, 0.276),
     'L0_gnn_bk': (0.0, 0.8),
     'L0_gnn_bv': (0.0, 0.1),
     'L0_gnn_bo': (0.0, 0.1),
     'L1_gnn_bq': (0.0, 0.8),
     'L1_gnn_bk': (0.0, 0.8),
     'L1_gnn_bv': (0.0, 0.1)}
    factors = {}
    for name, (base, spread) in spreads.items():
        noise = np.random.default_rng([zlib.crc32(name.encode()), seed]).standard_normal(out[name].shape)
        drawn = base * np.exp(spread * noise) if base else spread * noise
        out[name] = jnp.asarray(drawn.astype(out[name].dtype))
    for name, factor in factors.items():
        out[name] = (out[name] * factor).astype(out[name].dtype)
    return out
```

```python
from contextlib import ExitStack

import concourse.bass as bass
from concourse import mybir

F32 = mybir.dt.float32
F32R = mybir.dt.float32r
ALU = mybir.AluOpType
ACT = mybir.ActivationFunctionType

P = 128
NODES = 128
D = 512
H = 8
HD = D // H
NC = D // P
GB = 2
T = GB * NODES
SCALE = 1.0 / 8.0
EPS = 1e-5
MASKED = -1000000000.0
BIG = 3.0e38
WEIGHTS = ["q0", "k0", "v0", "o0", "q1", "k1", "v1"]
N_STAGE = 5
FIRST_W = 6

assert HD * 2 == P and NC * 2 == H


def adj_resnorm_kernel(nc, x_tok, x_feat, adj, wts, biases, out):
    G = x_feat.shape[0]

    def live(group):
        return not isinstance(group, int) or 0 <= group < G

    with ExitStack() as ctx:
        def sb(name, shape, dt=F32):
            return ctx.enter_context(nc.sbuf_tensor(name, shape, dt))

        def ps(name, shape):
            return ctx.enter_context(nc.psum_tensor(name, shape, F32))

        def sem(name):
            return ctx.enter_context(nc.semaphore(name))

        w_hi = {n: sb(f"w_hi_{n}", [P, NC, D], F32R) for n in WEIGHTS}
        w_lo = {n: sb(f"w_lo_{n}", [P, NC, D], F32R) for n in WEIGHTS}
        xt_raw = sb("xt_raw", [P, NC, T])
        xt_hi = [sb(f"xt_hi{l}", [P, NC, T], F32R) for l in range(2)]
        xt_lo = [sb(f"xt_lo{l}", [P, NC, T], F32R) for l in range(2)]
        q_t = [sb(f"q_t{l}", [P, NC, T]) for l in range(2)]
        k_t = [sb(f"k_t{l}", [P, NC, T]) for l in range(2)]
        v = [sb(f"v{l}", [P, GB, D]) for l in range(2)]
        x_res = sb("x_res", [P, GB, D])
        x1 = sb("x1", [P, GB, D])
        x1_res = sb("x1_res", [P, GB, D])
        prob = [sb(f"prob{b}", [P, 2, NC, NODES]) for b in range(GB)]
        prob_t = sb("prob_t", [P, 2, NC, NODES])
        at_hi = sb("at_hi", [P, NC, NODES], F32R)
        at_lo = sb("at_lo", [P, NC, NODES], F32R)
        y = sb("y", [P, GB, D])
        ident = sb("ident", [P, P])
        mask = [sb(f"mask{l}", [P, NODES]) for l in range(2)]
        bo_row = sb("bo_row", [P, D])
        bv1_row = sb("bv1_row", [P, D])
        bq_col = [sb(f"bq_col{l}", [P, NC]) for l in range(2)]
        bk_col = [sb(f"bk_col{l}", [P, NC]) for l in range(2)]
        bv0_col = sb("bv0_col", [P, NC])
        bq_scaled = [sb(f"bq_scaled{l}", [P, NC]) for l in range(2)]
        neg_max = [[sb(f"neg_max{l}{b}", [P, 2, NC]) for b in range(GB)] for l in range(2)]
        row_sum = [[sb(f"row_sum{l}{b}", [P, 2, NC]) for b in range(GB)] for l in range(2)]
        inv_sum = [[sb(f"inv_sum{l}{b}", [P, 2, NC]) for b in range(GB)] for l in range(2)]
        stats = [sb(f"stats{l}", [P, GB, 6]) for l in range(2)]
        mean_var = [sb(f"mean_var{l}", [P, GB, 2]) for l in range(2)]
        var_eps = [sb(f"var_eps{l}", [P, GB]) for l in range(2)]
        rstd = [sb(f"rstd{l}", [P, GB]) for l in range(2)]
        minus_half = sb("minus_half", [P, 1])

        stage = [prob[0], prob[1], prob_t, q_t[1], k_t[1]]
        stage = [s[:].rearrange("p a b c -> p (a b c)") if len(s.shape) == 4 else s[:].rearrange("p a b -> p (a b)")
                 for s in stage]

        ps_proj = [ps(f"ps_proj{i}", [P, 512]) for i in range(2)]
        ps_score = [ps(f"ps_score{e}", [P, NC, NODES]) for e in range(2)]
        ps_probt = ps("ps_probt", [P, 2, NC, NODES])
        ps_att = ps("ps_att", [P, 512])
        ps_x1t = ps("ps_x1t", [P, NC, NODES])

        staged = [sem(f"staged{i}") for i in range(N_STAGE)]
        w_hi_set = sem("w_hi_set")
        w_lo_set = sem("w_lo_set")
        small_in = sem("small_in")
        consts_set = sem("consts_set")
        dve_passed = sem("dve_passed")
        mask_step = sem("mask_step")
        ident_set = sem("ident_set")
        bv_split = sem("bv_split")
        bv_wo_done = sem("bv_wo_done")
        bo_set = sem("bo_set")
        raw_in = sem("raw_in")
        x_in = sem("x_in")
        y_out = [sem(f"y_out{b}") for b in range(GB)]
        x0_hi_set = sem("x0_hi_set")
        x0_lo_set = sem("x0_lo_set")
        x_res_set = sem("x_res_set")
        qk_done = [sem(f"qk_done{l}") for l in range(2)]
        qk_set = [sem(f"qk_set{l}") for l in range(2)]
        v_done = [sem(f"v_done{l}") for l in range(2)]
        v_set = [sem(f"v_set{l}") for l in range(2)]
        score_done = [sem(f"score_done{l}") for l in range(2)]
        masked_set = [sem(f"masked_set{l}") for l in range(2)]
        exp_set = [sem(f"exp_set{l}") for l in range(2)]
        inv_set = [sem(f"inv_set{l}") for l in range(2)]
        norm_set = sem("norm_set")
        probt_done = [sem(f"probt_done{l}") for l in range(2)]
        probt_set = [sem(f"probt_set{l}") for l in range(2)]
        att_done = [sem(f"att_done{l}") for l in range(2)]
        at_hi_set = sem("at_hi_set")
        at_lo_set = sem("at_lo_set")
        wo_done = sem("wo_done")
        y_norm_set = sem("y_norm_set")
        sum_set = [sem(f"sum_set{l}") for l in range(2)]
        stats_set = [sem(f"stats_set{l}") for l in range(2)]
        mean_set = [sem(f"mean_set{l}") for l in range(2)]
        eps_set = [sem(f"eps_set{l}") for l in range(2)]
        rstd_set = [sem(f"rstd_set{l}") for l in range(2)]
        ln_set = [sem(f"ln_set{l}") for l in range(2)]
        x1t_done = sem("x1t_done")
        x1_hi_set = sem("x1_hi_set")
        x1_lo_set = sem("x1_lo_set")
        x1_res_set = sem("x1_res_set")

        def need(eng, semaphore, value):
            if not isinstance(value, int) or value > 0:
                eng.wait_ge(semaphore, value)

        def steps(eng, phase_a, phase_b, between=None):
            for g in range(3):
                phase_a(g)
                if g == 0 and between:
                    between()
                phase_b(g)
            with eng.Fori(3, G) as g:
                phase_a(g)
                phase_b(g)
            for g in range(G, G + 2):
                phase_a(g)
                phase_b(g)

        def emptied(g, u):
            if u < 6:
                return live(g) and ((qk_set[0], g * 4 + u + 1) if u < 4 else (v_set[0], g * 2 + u - 3))
            if u in (11, 13):
                return live(g) and (sum_set[0], g * 2 + (u - 11) // 2 + 1)
            if u < 10:
                return live(g - 1) and (qk_set[1], (g - 1) * 4 + u - 5)
            return live(g - 1) and (v_set[1], (g - 1) * 2 + (1 if u == 10 else 2))

        def need_bank(eng, g, u):
            for back in range(2, 14, 2):
                s, n = (g, u - back) if u >= back else (g - 1, u - back + 14)
                if isinstance(s, int) and s < 0:
                    return
                last = emptied(s, n)
                if last:
                    eng.wait_ge(*last)
                    return

        block = ctx.enter_context(nc.Block())

        @block.sync
        def _(sp):
            sp.dma_start(xt_raw[:], x_feat[0]).then_inc(raw_in, 16)
            halves = [(n, half) for n in WEIGHTS for half in range(2)]
            for i, (n, half) in enumerate(halves):
                if i >= N_STAGE:
                    sp.wait_ge(w_hi_set, i - N_STAGE + 1)
                    sp.wait_ge(w_lo_set, i - N_STAGE + 1)
                sp.dma_start(stage[i % N_STAGE].rearrange("p (c n) -> p c n", c=2),
                             wts[n].rearrange("(c p) n -> p c n", p=P)[:, 2 * half:2 * half + 2, :]
                             ).then_inc(staged[i % N_STAGE], 16)
                if i == FIRST_W:
                    sp.dma_start(x_res[:], x_tok[0]).then_inc(x_in, 16)

            def phase_a(g):
                if live(g + 1) and not (isinstance(g, int) and g + 1 >= G):
                    load_raw(g + 1)
                if live(g) and not (isinstance(g, int) and g == 0):
                    need(sp, ln_set[0], g * 2)
                    sp.dma_start(x_res[:], x_tok[g]).then_inc(x_in, 16)
                if live(g - 2):
                    store(g - 2, 0)

            def load_raw(g):
                need(sp, x0_hi_set, g)
                need(sp, x0_lo_set, g)
                sp.dma_start(xt_raw[:], x_feat[g]).then_inc(raw_in, 16)

            def store(j, b):
                sp.wait_ge(ln_set[1], j * 2 + b + 1)
                sp.dma_start(out[j, b], y[:, b, :]).then_inc(y_out[b], 16)

            def phase_b(g):
                if live(g - 2):
                    store(g - 2, 1)

            for g in range(3):
                phase_a(g)
                phase_b(g)
            with sp.Fori(3, G - 1) as g:
                phase_a(g)
                phase_b(g)
            for g in range(G - 1, G + 2):
                phase_a(g)
                phase_b(g)
            for b in range(GB):
                sp.wait_ge(y_out[b], 16 * G)

        @block.tensor
        def _(pe):
            def project_t(l, ps_out, w, chunks, done):
                for i, m in enumerate(chunks):
                    cols = slice(m * P, m * P + P)
                    for c in range(NC):
                        parts = [(w_hi[w], xt_hi[l]), (w_hi[w], xt_lo[l]), (w_lo[w], xt_hi[l])]
                        for n, (wp, xp) in enumerate(parts):
                            last = pe.matmul(ps_out[:, i * T:(i + 1) * T], wp[:, c, cols], xp[:, c, :],
                                             start=(c == 0 and n == 0), stop=(c == NC - 1 and n == 2))
                last.then_inc(done, 1)

            def project(ps_out, hi, lo, w, done):
                for c in range(NC):
                    parts = [(hi(c), w_hi[w]), (hi(c), w_lo[w]), (lo(c), w_hi[w])]
                    for n, (xp, wp) in enumerate(parts):
                        last = pe.matmul(ps_out[:, :], xp, wp[:, c, :],
                                         start=(c == 0 and n == 0), stop=(c == NC - 1 and n == 2))
                last.then_inc(done, 1)

            def unit(l, g, u, group, i):
                need_bank(pe, g, u)
                bank = ps_proj[u % 2]
                if i < 4:
                    project_t(l, bank, ("q" if i < 2 else "k") + str(l), (2 * (i % 2), 2 * (i % 2) + 1), qk_done[l])
                else:
                    tok = slice((i - 4) * NODES, (i - 3) * NODES)
                    project(bank, lambda c: xt_hi[l][:, c, tok], lambda c: xt_lo[l][:, c, tok], f"v{l}", v_done[l])

            def scores(l, group, b, bank_free):
                tok = slice(b * NODES, (b + 1) * NODES)
                for e in range(2):
                    if bank_free:
                        need(pe, bank_free[0], bank_free[1] + e)
                    rows = slice(e * HD, (e + 1) * HD)
                    for c in range(NC):
                        last = pe.matmul(ps_score[e][:, c, :], q_t[l][rows, c, tok], k_t[l][rows, c, tok],
                                         start=True, stop=True)
                    last.then_inc(score_done[l], 1)

            def transpose_probs(l, b, ready, first):
                for e in range(2):
                    pe.wait_ge(ready, first + e)
                    for c in range(NC):
                        last = pe.transpose(ps_probt[:, e, c, :], prob[b][:, e, c, :], ident[:])
                last.then_inc(probt_done[l], 1)

            def attend0(b):
                for c in range(NC):
                    for e in range(2):
                        h = 2 * c + e
                        last = pe.matmul(ps_att[e * HD:(e + 1) * HD, c * NODES:(c + 1) * NODES],
                                         v[0][:, b, h * HD:(h + 1) * HD], prob_t[:, e, c, :], start=True, stop=True)
                last.then_inc(att_done[0], 1)

            def attend1(b):
                for c in range(NC):
                    for e in range(2):
                        h = 2 * c + e
                        last = pe.matmul(ps_att[:, h * HD:(h + 1) * HD], prob_t[:, e, c, :],
                                         v[1][:, b, h * HD:(h + 1) * HD], start=True, stop=True)
                last.then_inc(att_done[1], 1)

            def transpose_x1(m, b):
                pe.wait_ge(ln_set[0], m * 2 + b + 1)
                need(pe, x1_hi_set, m * 2 + b)
                need(pe, x1_lo_set, m * 2 + b)
                for c in range(NC):
                    last = pe.transpose(ps_x1t[:, c, :], x1[:, b, c * P:(c + 1) * P], ident[:])
                last.then_inc(x1t_done, 1)

            def phase_a(g):
                j, m = g - 2, g - 1
                att, proj, xt = live(j), live(g), live(m)

                def layer0_unit(i):
                    if proj:
                        if i == 0:
                            pe.wait_ge(x0_hi_set, g + 1)
                            pe.wait_ge(x0_lo_set, g + 1)
                        if isinstance(g, int) and g == 0 and i % 2 == 0:
                            pe.wait_ge(w_hi_set, i + 2)
                            pe.wait_ge(w_lo_set, i + 2)
                        unit(0, g, i, g, i)

                if att:
                    if isinstance(g, int) and g == 2:
                        pe.wait_ge(ident_set, 2)
                    pe.wait_ge(qk_set[1], j * 4 + 4)
                    scores(1, j, 0, (masked_set[0], g * 4 - 1) if live(m) else (masked_set[1], j * 4 - 1))
                layer0_unit(0)
                layer0_unit(1)
                if xt:
                    transpose_x1(m, 0)
                if att:
                    scores(1, j, 1, (masked_set[1], j * 4 + 1))
                    need(pe, *((probt_set[0], g * 2) if live(m) else (probt_set[1], j * 2)))
                    transpose_probs(1, 0, exp_set[1], j * 4 + 1)
                layer0_unit(2)
                if xt:
                    transpose_x1(m, 1)
                if att:
                    pe.wait_ge(probt_set[1], j * 2 + 1)
                    pe.wait_ge(v_set[1], j * 2 + 1)
                    if live(m):
                        need(pe, at_hi_set, g * 2)
                        need(pe, at_lo_set, g * 2)
                    else:
                        need(pe, y_norm_set, j * 2)
                    attend1(0)
                layer0_unit(3)
                if att:
                    pe.wait_ge(probt_set[1], j * 2 + 1)
                    transpose_probs(1, 1, exp_set[1], j * 4 + 3)
                layer0_unit(4)
                if att:
                    pe.wait_ge(probt_set[1], j * 2 + 2)
                    pe.wait_ge(v_set[1], j * 2 + 2)
                    pe.wait_ge(y_norm_set, j * 2 + 1)
                    attend1(1)
                layer0_unit(5)

            def phase_b(g):
                j, m = g - 2, g - 1
                att, proj = live(g), live(m)

                def layer1_unit(i):
                    if proj:
                        if i == 0:
                            pe.wait_ge(x1_hi_set, m * 2 + 2)
                            pe.wait_ge(x1_lo_set, m * 2 + 2)
                        unit(1, g, (6, 7, 8, 9, 10, 12)[i], m, i)

                def wo(b):
                    pe.wait_ge(at_hi_set, g * 2 + b + 1)
                    pe.wait_ge(at_lo_set, g * 2 + b + 1)
                    u = 11 + 2 * b
                    need_bank(pe, g, u)
                    project(ps_proj[u % 2], lambda c: at_hi[:, c, :], lambda c: at_lo[:, c, :], "o0", wo_done)

                if att:
                    pe.wait_ge(qk_set[0], g * 4 + 4)
                    scores(0, g, 0, (masked_set[1], j * 4 + 3) if live(j) else (masked_set[0], g * 4 - 1))
                layer1_unit(0)
                layer1_unit(1)
                if att:
                    scores(0, g, 1, (masked_set[0], g * 4 + 1))
                    need(pe, *((probt_set[1], j * 2 + 2) if live(j) else (probt_set[0], g * 2)))
                    transpose_probs(0, 0, norm_set, g * 4 + 1)
                layer1_unit(2)
                if att:
                    pe.wait_ge(probt_set[0], g * 2 + 1)
                    pe.wait_ge(v_set[0], g * 2 + 1)
                    if live(j):
                        pe.wait_ge(y_norm_set, j * 2 + 2)
                    else:
                        need(pe, at_hi_set, g * 2)
                        need(pe, at_lo_set, g * 2)
                    attend0(0)
                layer1_unit(3)
                if att:
                    transpose_probs(0, 1, norm_set, g * 4 + 3)
                layer1_unit(4)
                if att:
                    wo(0)
                    pe.wait_ge(probt_set[0], g * 2 + 2)
                    pe.wait_ge(v_set[0], g * 2 + 2)
                    attend0(1)
                layer1_unit(5)
                if att:
                    wo(1)

            def bias_product():
                pe.wait_ge(ident_set, 2)
                pe.wait_ge(bv_split, 2)
                pe.wait_ge(w_hi_set, 2 * len(WEIGHTS))
                pe.wait_ge(w_lo_set, 2 * len(WEIGHTS))
                project(ps_att, lambda c: at_hi[:, c, :], lambda c: at_lo[:, c, :], "o0", bv_wo_done)
                pe.wait_ge(bo_set, 1)

            steps(pe, phase_a, phase_b, bias_product)

        @block.scalar
        def _(act):
            small = [(bq_col[0], "bq0"), (bk_col[0], "bk0"), (bv0_col, "bv0"), (bq_col[1], "bq1"), (bk_col[1], "bk1")]
            for tile, n in small:
                act.dma_start(tile[:], biases[n + "_col"]).then_inc(small_in, 16)
            for tile, n in ((bo_row, "bo0"), (bv1_row, "bv1")):
                act.dma_start(tile[:], biases[n].rearrange("(a n) -> a n", a=1).to_broadcast([P, D])
                              ).then_inc(small_in, 16)
            for tile in mask:
                act.dma_start(tile[:], adj).then_inc(small_in, 16)
            halves = [(n, half) for n in WEIGHTS for half in range(2)]
            for i, (n, half) in enumerate(halves[:FIRST_W]):
                act.wait_ge(staged[i % N_STAGE], 16 * (i // N_STAGE + 1))
                act.activation(w_hi[n][:, 2 * half:2 * half + 2, :].rearrange("p c n -> p (c n)"),
                               stage[i % N_STAGE], ACT.Copy).then_inc(w_hi_set, 1)

            def qk_out(l, g, u, group, i, freed_by, times):
                act.wait_ge(qk_done[l], group * 4 + i + 1)
                need(act, freed_by, times)
                tile = q_t[l] if i < 2 else k_t[l]
                bias = bq_scaled[l] if i < 2 else bk_col[l]
                for n in range(2):
                    m = 2 * (i % 2) + n
                    last = act.activation(tile[:, m, :], ps_proj[u % 2][:, n * T:(n + 1) * T], ACT.Identity,
                                          bias=bias[:, m:m + 1], scale=SCALE if i < 2 else 1.0)
                last.then_inc(qk_set[l], 1)

            def v_out(l, u, group, b):
                act.wait_ge(v_done[l], group * 2 + b + 1)
                need(act, att_done[l], group * 2)
                act.activation(v[l][:, b, :], ps_proj[u % 2][:, :], ACT.Copy).then_inc(v_set[l], 1)

            def exps(l, group, b):
                for e in range(2):
                    act.wait_ge(masked_set[l], group * 4 + 2 * b + e + 1)
                    for c in range(NC):
                        last = act.activation(prob[b][:, e, c, :], prob[b][:, e, c, :], ACT.Exp,
                                              bias=neg_max[l][b][:, e, c:c + 1], scale=-1.0,
                                              accum_out=row_sum[l][b][:, e, c:c + 1])
                    last.then_inc(exp_set[l], 1)

            def probt_out(l, group, b, freed_by, times):
                act.wait_ge(probt_done[l], group * 2 + b + 1)
                need(act, freed_by, times)
                act.activation(prob_t[:].rearrange("p e c n -> p (e c n)"),
                               ps_probt[:].rearrange("p e c n -> p (e c n)"), ACT.Copy).then_inc(probt_set[l], 1)

            def phase_a(g):
                j, m = g - 2, g - 1
                att, proj, xt = live(j), live(g), live(m)

                def q_or_k(i):
                    if proj:
                        qk_out(0, g, i, g, i, score_done[0], g * 4)

                def x1_hi(b):
                    if xt:
                        act.wait_ge(x1t_done, m * 2 + b + 1)
                        need(act, qk_done[1], m * 4)
                        need(act, v_done[1], m * 2)
                        act.activation(xt_hi[1][:, :, b * NODES:(b + 1) * NODES], ps_x1t[:], ACT.Copy
                                       ).then_inc(x1_hi_set, 1)

                if isinstance(g, int) and g == 0:
                    act.wait_ge(consts_set, 1)
                if att:
                    exps(1, j, 0)
                q_or_k(0)
                q_or_k(1)
                x1_hi(0)
                if att:
                    probt_out(1, j, 0, *((att_done[0], g * 2) if live(m) else (att_done[1], j * 2)))
                    exps(1, j, 1)
                q_or_k(2)
                x1_hi(1)
                q_or_k(3)
                if att:
                    probt_out(1, j, 1, att_done[1], j * 2 + 1)
                if proj:
                    v_out(0, 4, g, 0)
                    v_out(0, 5, g, 1)

            def phase_b(g):
                j, m = g - 2, g - 1
                att, proj = live(g), live(m)

                def q_or_k(i):
                    if proj:
                        qk_out(1, g, 6 + i, m, i, score_done[1], m * 4)

                def at_high(b):
                    if att:
                        act.wait_ge(att_done[0], g * 2 + b + 1)
                        need(act, wo_done, g * 2 + b)
                        act.activation(at_hi[:].rearrange("p c n -> p (c n)"), ps_att[:], ACT.Copy
                                       ).then_inc(at_hi_set, 1)

                if att:
                    exps(0, g, 0)
                q_or_k(0)
                q_or_k(1)
                if att:
                    probt_out(0, g, 0, *((att_done[1], j * 2 + 2) if live(j) else (att_done[0], g * 2)))
                    exps(0, g, 1)
                q_or_k(2)
                at_high(0)
                q_or_k(3)
                if att:
                    probt_out(0, g, 1, att_done[0], g * 2 + 1)
                if proj:
                    v_out(1, 10, m, 0)
                at_high(1)
                if proj:
                    v_out(1, 12, m, 1)

            steps(act, phase_a, phase_b)

        @block.vector
        def _(dve):
            halves = [(n, half) for n in WEIGHTS for half in range(2)]

            def weight_low(i):
                n, half = halves[i]
                hi = w_hi[n][:, 2 * half:2 * half + 2, :].rearrange("p c n -> p (c n)")
                if i >= FIRST_W:
                    dve.wait_ge(staged[i % N_STAGE], 16 * (i // N_STAGE + 1))
                    dve.tensor_copy(hi, stage[i % N_STAGE]).then_inc(w_hi_set, 1)
                dve.wait_ge(w_hi_set, i + 1)
                dve.tensor_tensor(w_lo[n][:, 2 * half:2 * half + 2, :].rearrange("p c n -> p (c n)"),
                                  stage[i % N_STAGE], hi.bitcast(F32), ALU.subtract).then_inc(w_lo_set, 1)

            def x0_high(group):
                dve.wait_ge(raw_in, (group + 1) * 16)
                dve.tensor_copy(xt_hi[0][:], xt_raw[:]).then_inc(x0_hi_set, 1)

            dve.wait_ge(small_in, 16 * 9)
            for l in range(2):
                dve.tensor_scalar(bq_scaled[l][:], bq_col[l][:], SCALE, None, ALU.mult)
            dve.tensor_scalar(mask[0][:], mask[0][:], -1.0, 1.0, ALU.mult, ALU.add).then_inc(mask_step, 1)
            dve.wait_ge(mask_step, 1)
            dve.tensor_scalar(mask[0][:], mask[0][:], MASKED, None, ALU.mult).then_inc(mask_step, 1)
            dve.tensor_scalar(mask[1][:], mask[1][:], 0.0, MASKED, ALU.is_equal, ALU.mult).then_inc(mask_step, 1)
            dve.wait_ge(mask_step, 3)
            dve.tensor_copy(at_hi[:], bv0_col[:].unsqueeze(2).to_broadcast([P, NC, NODES])).then_inc(bv_split, 1)
            dve.wait_ge(bv_split, 1)
            dve.tensor_tensor(at_lo[:], bv0_col[:].unsqueeze(2).to_broadcast([P, NC, NODES]),
                              at_hi[:].bitcast(F32), ALU.subtract).then_inc(bv_split, 1)
            dve.memset(minus_half[:], -0.5).then_inc(consts_set, 1)
            x0_high(0)
            for i in range(FIRST_W):
                weight_low(i)

            def mask_scores(l, group, b, prob_free, n_free):
                need(dve, prob_free, n_free)
                for e in range(2):
                    dve.wait_ge(score_done[l], group * 4 + 2 * b + e + 1)
                    dve.sem_inc(dve_passed, 1)
                    for c in range(NC):
                        last = dve.tensor_tensor_reduce(prob[b][:, e, c, :], ps_score[e][:, c, :], mask[l][:],
                                                        -1.0, BIG, ALU.add, ALU.min,
                                                        neg_max[l][b][:, e, c:c + 1])
                    last.then_inc(masked_set[l], 1)

            def invert_sums(l, group, b):
                for e in range(2):
                    dve.wait_ge(exp_set[l], group * 4 + 2 * b + e + 1)
                    dve.reciprocal(inv_sum[l][b][:, e, :], row_sum[l][b][:, e, :]).then_inc(inv_set[l], 1)

            def statistics(l, group, b):
                done = group * 2 + b + 1
                row = (x_res if l == 0 else y)[:, b, :]
                dve.wait_ge(sum_set[l], done)
                dve.bn_stats(stats[l][:, b, :], row).then_inc(stats_set[l], 1)
                dve.wait_ge(stats_set[l], done)
                dve.sem_inc(dve_passed, 1)
                dve.bn_aggr(mean_var[l][:, b, :], stats[l][:, b, :]).then_inc(mean_set[l], 1)
                dve.wait_ge(mean_set[l], done)
                dve.tensor_scalar(var_eps[l][:, b:b + 1], mean_var[l][:, b, 1:2], EPS, None, ALU.add
                                  ).then_inc(eps_set[l], 1)

            def normalise(l, group, b):
                done = group * 2 + b + 1
                dve.wait_ge(rstd_set[l], done)
                if l == 0:
                    need(dve, x1t_done, done - 2)
                    need(dve, x1_res_set, done - 2)
                src, dst = (x_res, x1) if l == 0 else (y, y)
                dve.tensor_scalar(dst[:, b, :], src[:, b, :], mean_var[l][:, b, 0:1], rstd[l][:, b:b + 1],
                                  ALU.subtract, ALU.mult).then_inc(ln_set[l], 1)

            def x1_low(m, b):
                dve.wait_ge(x1_hi_set, m * 2 + b + 1)
                tok = slice(b * NODES, (b + 1) * NODES)
                dve.tensor_tensor(xt_lo[1][:, :, tok], ps_x1t[:], xt_hi[1][:, :, tok].bitcast(F32), ALU.subtract
                                  ).then_inc(x1_lo_set, 1)

            def residual1(j, b):
                dve.wait_ge(att_done[1], j * 2 + b + 1)
                dve.wait_ge(inv_set[1], j * 4 + 2 * b + 2)
                if not isinstance(j, int) or j > 0:
                    dve.wait_ge(y_out[b], j * 16)
                heads = "p (c e d) -> p c e d"
                dve.tensor_tensor(y[:, b, :].rearrange(heads, e=2, d=HD), ps_att[:].rearrange(heads, e=2, d=HD),
                                  inv_sum[1][b][:].rearrange("p e c -> p c e").unsqueeze(3).to_broadcast([P, NC, 2, HD]),
                                  ALU.mult).then_inc(y_norm_set, 1)
                dve.wait_ge(y_norm_set, j * 2 + b + 1)
                dve.wait_ge(x1_res_set, j * 2 + b + 1)
                dve.tensor_tensor(y[:, b, :], y[:, b, :], x1_res[:, b, :], ALU.add).then_inc(sum_set[1], 1)

            def at_low(g, b):
                dve.wait_ge(at_hi_set, g * 2 + b + 1)
                dve.tensor_tensor(at_lo[:].rearrange("p c n -> p (c n)"), ps_att[:],
                                  at_hi[:].rearrange("p c n -> p (c n)").bitcast(F32), ALU.subtract
                                  ).then_inc(at_lo_set, 1)

            def residual0(g, b):
                dve.wait_ge(wo_done, g * 2 + b + 1)
                dve.wait_ge(x_res_set, g + 1)
                dve.tensor_tensor(x_res[:, b, :], ps_proj[1][:, :], x_res[:, b, :], ALU.add).then_inc(sum_set[0], 1)

            def phase_a(g):
                j, m = g - 2, g - 1
                if live(j):
                    mask_scores(1, j, 0, *((probt_done[0], m * 2 + 1) if live(m) else (probt_done[1], j * 2 - 1)))
                if live(m):
                    normalise(0, m, 1)
                    x1_low(m, 0)
                if live(j):
                    mask_scores(1, j, 1, *((probt_done[0], m * 2 + 2) if live(m) else (probt_done[1], j * 2)))
                if live(m):
                    x1_low(m, 1)
                if live(j):
                    invert_sums(1, j, 0)
                    residual1(j, 0)
                    statistics(1, j, 0)
                    invert_sums(1, j, 1)
                    normalise(1, j, 0)
                    residual1(j, 1)
                    statistics(1, j, 1)

            def phase_b(g):
                j = g - 2
                att = live(g)
                if att:
                    mask_scores(0, g, 0, *((probt_done[1], j * 2 + 1) if live(j) else (probt_done[0], g * 2 - 1)))
                if live(j):
                    normalise(1, j, 1)
                if att:
                    invert_sums(0, g, 0)
                    if not isinstance(g, int) or g + 1 < G:
                        dve.wait_ge(qk_done[0], g * 4 + 4)
                        dve.wait_ge(v_done[0], g * 2 + 2)
                        x0_high(g + 1)
                    mask_scores(0, g, 1, *((probt_done[1], j * 2 + 2) if live(j) else (probt_done[0], g * 2)))
                    invert_sums(0, g, 1)
                    at_low(g, 0)
                    residual0(g, 0)
                    at_low(g, 1)
                    statistics(0, g, 0)
                    normalise(0, g, 0)
                    residual0(g, 1)
                    statistics(0, g, 1)

            def other_weights():
                for i in range(FIRST_W, len(halves)):
                    weight_low(i)
                dve.wait_ge(bv_wo_done, 1)
                dve.tensor_tensor(bo_row[:], ps_att[:], bo_row[:], ALU.add).then_inc(bo_set, 1)

            for g in range(3):
                phase_a(g)
                if g == 0:
                    other_weights()
                phase_b(g)
            with dve.Fori(3, G - 1) as g:
                phase_a(g)
                phase_b(g)
            for g in range(G - 1, G + 2):
                phase_a(g)
                phase_b(g)

        @block.gpsimd
        def _(pool):
            pool.memset(ident[:], 0.0).then_inc(ident_set, 1)
            pool.wait_ge(ident_set, 1)
            pool.affine_select(out=ident[:], in_=ident[:], compare_op=ALU.not_equal, fill=1.0, base=0,
                               pattern=[[-1, P]], channel_multiplier=1).then_inc(ident_set, 1)

            def x0_low(group):
                pool.wait_ge(x0_hi_set, group + 1)
                pool.tensor_tensor(xt_lo[0][:], xt_raw[:], xt_hi[0][:].bitcast(F32), ALU.subtract
                                   ).then_inc(x0_lo_set, 1)

            def inverse_deviation(l, group, b):
                done = group * 2 + b + 1
                pool.wait_ge(eps_set[l], done)
                need(pool, ln_set[l], done - 2)
                pool.tensor_tensor(rstd[l][:, b:b + 1], var_eps[l][:, b:b + 1], minus_half[:], ALU.pow
                                   ).then_inc(rstd_set[l], 1)

            def normalise_probs(g, b):
                for e in range(2):
                    pool.wait_ge(inv_set[0], g * 4 + 2 * b + e + 1)
                    pool.tensor_tensor(prob[b][:, e], prob[b][:, e],
                                       inv_sum[0][b][:, e, :].unsqueeze(2).to_broadcast([P, NC, NODES]), ALU.mult
                                       ).then_inc(norm_set, 1)

            def copy_x1(m, b):
                pool.wait_ge(ln_set[0], m * 2 + b + 1)
                need(pool, sum_set[1], m * 2 + b - 1)
                pool.tensor_tensor(x1_res[:, b, :], x1[:, b, :], bv1_row[:], ALU.add).then_inc(x1_res_set, 1)

            def phase_a(g):
                j, m = g - 2, g - 1
                if live(m):
                    inverse_deviation(0, m, 1)
                if live(j):
                    inverse_deviation(1, j, 0)
                if live(g):
                    pool.wait_ge(x_in, (g + 1) * 16)
                    if isinstance(g, int) and g == 0:
                        pool.wait_ge(bo_set, 1)
                    pool.tensor_tensor(x_res[:], x_res[:], bo_row[:].unsqueeze(1).to_broadcast([P, GB, D]), ALU.add
                                       ).then_inc(x_res_set, 1)
                if live(j):
                    inverse_deviation(1, j, 1)

            def phase_b(g):
                m = g - 1
                if live(g):
                    normalise_probs(g, 0)
                if live(m):
                    copy_x1(m, 0)
                    copy_x1(m, 1)
                if live(g):
                    normalise_probs(g, 1)
                    if not isinstance(g, int) or g + 1 < G:
                        x0_low(g + 1)
                    inverse_deviation(0, g, 0)

            pool.wait_ge(consts_set, 1)
            x0_low(0)
            for g in range(3):
                phase_a(g)
                phase_b(g)
            with pool.Fori(3, G - 1) as g:
                phase_a(g)
                phase_b(g)
            for g in range(G - 1, G + 2):
                phase_a(g)
                phase_b(g)


def kernel(**inputs):
    import numpy as np
    import concourse.bacc as bacc
    from concourse.bass_utils import run_bass_kernel_spmd

    nc = bacc.Bacc("TRN2", target_bir_lowering=False, num_devices=1)
    x = np.asarray(inputs["x"])
    graphs = x.shape[0]
    groups = graphs // GB
    arrays = {
        "x_tok": np.ascontiguousarray(x.reshape(groups, GB, NODES, D).transpose(0, 2, 1, 3)),
        "x_feat": np.ascontiguousarray(x.reshape(groups, T, NC, P).transpose(0, 3, 2, 1)),
        "adj": np.ascontiguousarray(inputs["adj"]),
    }
    names = {"q0": "L0_gnn_Wq", "k0": "L0_gnn_Wk", "v0": "L0_gnn_Wv", "o0": "L0_gnn_Wo",
             "q1": "L1_gnn_Wq", "k1": "L1_gnn_Wk", "v1": "L1_gnn_Wv"}
    for short, name in names.items():
        arrays[f"w_{short}"] = np.ascontiguousarray(inputs[name])
        bias = np.asarray(inputs[name.replace("_W", "_b")])
        arrays[f"b_{short}"] = np.ascontiguousarray(bias)
        arrays[f"b_{short}_col"] = np.ascontiguousarray(bias.reshape(NC, P).T)
    aps = {n: nc.dram_tensor(n, a.shape, mybir.dt.from_np(a.dtype), kind="ExternalInput").ap()
           for n, a in arrays.items()}
    out = nc.dram_tensor("out", (groups, GB, NODES, D), F32, kind="ExternalOutput").ap()
    adj_resnorm_kernel(nc, aps["x_tok"], aps["x_feat"], aps["adj"], {s: aps[f"w_{s}"] for s in names},
                       {n.replace("b_", "b"): ap for n, ap in aps.items() if n.startswith("b_")}, out)
    result = run_bass_kernel_spmd(nc, [arrays], core_ids=[0])
    return result.results[0]["out"].reshape(graphs, NODES, D)
```

```python
from contextlib import ExitStack

import concourse.bass as bass
from concourse import mybir

F32 = mybir.dt.float32
F32R = mybir.dt.float32r
ALU = mybir.AluOpType
ACT = mybir.ActivationFunctionType

P = 128
NODES = 128
D = 512
H = 8
HD = D // H
NC = D // P
GB = 2
T = GB * NODES
SCALE = 1.0 / 8.0
EPS = 1e-5
SQ = 32
BLK = P // SQ
MASKED = -1000000000.0
BIG = 3.0e38
WEIGHTS = ["q0", "k0", "v0", "o0", "q1", "k1", "v1"]
N_STAGE = 5
FIRST_W = 6

assert HD * 2 == P and NC * 2 == H


def adj_resnorm_kernel(nc, x_tok, x_feat, adj, wts, biases, out):
    G = x_feat.shape[0]

    def live(group):
        return not isinstance(group, int) or 0 <= group < G

    with ExitStack() as ctx:
        def sb(name, shape, dt=F32):
            return ctx.enter_context(nc.sbuf_tensor(name, shape, dt))

        def ps(name, shape):
            return ctx.enter_context(nc.psum_tensor(name, shape, F32))

        def sem(name):
            return ctx.enter_context(nc.semaphore(name))

        w_hi = {n: sb(f"w_hi_{n}", [P, NC, D], F32R) for n in WEIGHTS}
        w_lo = {n: sb(f"w_lo_{n}", [P, NC, D], F32R) for n in WEIGHTS}
        xt_raw = sb("xt_raw", [P, NC, T])
        xt_hi = [sb(f"xt_hi{l}", [P, NC, T], F32R) for l in range(2)]
        xt_lo = [sb(f"xt_lo{l}", [P, NC, T], F32R) for l in range(2)]
        q_t = [sb(f"q_t{l}", [P, NC, T]) for l in range(2)]
        k_t = [sb(f"k_t{l}", [P, NC, T]) for l in range(2)]
        v = [sb(f"v{l}", [P, GB, D]) for l in range(2)]
        x_res = sb("x_res", [P, GB, D])
        x1 = sb("x1", [P, GB, D])
        x1_res = sb("x1_res", [P, GB, D])
        prob = [sb(f"prob{b}", [P, 2, NC, NODES]) for b in range(GB)]
        blocks_t = sb("blocks_t", [P, BLK, 2, NC, SQ])
        prob_t = [sb(f"prob_t{b}", [P, BLK, 2, NC, SQ]) for b in range(GB)]
        at_hi = sb("at_hi", [P, NC, NODES], F32R)
        at_lo = sb("at_lo", [P, NC, NODES], F32R)
        at1 = sb("at1", [P, NC, NODES])
        y = sb("y", [P, GB, D])
        ident = sb("ident", [P, P])
        mask = [sb(f"mask{l}", [P, NODES]) for l in range(2)]
        bo_row = sb("bo_row", [P, D])
        bv1_row = sb("bv1_row", [P, D])
        bq_col = [sb(f"bq_col{l}", [P, NC]) for l in range(2)]
        bk_col = [sb(f"bk_col{l}", [P, NC]) for l in range(2)]
        bv0_col = sb("bv0_col", [P, NC])
        bq_scaled = [sb(f"bq_scaled{l}", [P, NC]) for l in range(2)]
        neg_max = [[sb(f"neg_max{l}{b}", [P, 2, NC]) for b in range(GB)] for l in range(2)]
        row_sum = [[sb(f"row_sum{l}{b}", [P, 2, NC]) for b in range(GB)] for l in range(2)]
        inv_sum = [[sb(f"inv_sum{l}{b}", [P, 2, NC]) for b in range(GB)] for l in range(2)]
        stats = [sb(f"stats{l}", [P, GB, 6]) for l in range(2)]
        mean_var = [sb(f"mean_var{l}", [P, GB, 2]) for l in range(2)]
        var_eps = [sb(f"var_eps{l}", [P, GB]) for l in range(2)]
        rstd = [sb(f"rstd{l}", [P, GB]) for l in range(2)]
        minus_half = sb("minus_half", [P, 1])

        stage = [s[:].rearrange("p a b c -> p (a b c)") for s in prob] + \
                [s[:].rearrange("p a b c d -> p (a b c d)") for s in (*prob_t, blocks_t)]

        ps_proj = [ps(f"ps_proj{i}", [P, 512]) for i in range(2)]
        ps_score = [ps(f"ps_score{e}", [P, NC, NODES]) for e in range(2)]
        ps_att = ps("ps_att", [P, 512])
        ps_back = ps("ps_back", [P, D])
        ps_x1t = ps("ps_x1t", [P, NC, NODES])

        staged = [sem(f"staged{i}") for i in range(N_STAGE)]
        w_hi_set = sem("w_hi_set")
        w_lo_set = sem("w_lo_set")
        small_in = sem("small_in")
        consts_set = sem("consts_set")
        dve_passed = sem("dve_passed")
        sp_passed = sem("sp_passed")
        mask_step = sem("mask_step")
        ident_set = sem("ident_set")
        bv_split = sem("bv_split")
        bv_wo_done = sem("bv_wo_done")
        bo_set = sem("bo_set")
        raw_in = sem("raw_in")
        x_in = sem("x_in")
        y_out = [sem(f"y_out{b}") for b in range(GB)]
        x0_hi_set = sem("x0_hi_set")
        x0_lo_set = sem("x0_lo_set")
        x_res_set = sem("x_res_set")
        qk_done = [sem(f"qk_done{l}") for l in range(2)]
        qk_set = [sem(f"qk_set{l}") for l in range(2)]
        v_done = [sem(f"v_done{l}") for l in range(2)]
        v_set = [sem(f"v_set{l}") for l in range(2)]
        score_done = [sem(f"score_done{l}") for l in range(2)]
        masked_set = [sem(f"masked_set{l}") for l in range(2)]
        exp_set = [sem(f"exp_set{l}") for l in range(2)]
        inv_set = [sem(f"inv_set{l}") for l in range(2)]
        norm_set = [sem(f"norm_set{l}") for l in range(2)]
        blocks_set = [sem(f"blocks_set{l}") for l in range(2)]
        probt_in = [sem(f"probt_in{l}") for l in range(2)]
        att_done = [sem(f"att_done{l}") for l in range(2)]
        at_hi_set = sem("at_hi_set")
        at_lo_set = sem("at_lo_set")
        wo_done = sem("wo_done")
        at1_set = sem("at1_set")
        back_done = sem("back_done")
        sum_set = [sem(f"sum_set{l}") for l in range(2)]
        stats_set = [sem(f"stats_set{l}") for l in range(2)]
        mean_set = [sem(f"mean_set{l}") for l in range(2)]
        eps_set = [sem(f"eps_set{l}") for l in range(2)]
        rstd_set = [sem(f"rstd_set{l}") for l in range(2)]
        ln_set = [sem(f"ln_set{l}") for l in range(2)]
        x1t_done = sem("x1t_done")
        x1_hi_set = sem("x1_hi_set")
        x1_lo_set = sem("x1_lo_set")
        x1_res_set = sem("x1_res_set")

        def need(eng, semaphore, value):
            if not isinstance(value, int) or value > 0:
                eng.wait_ge(semaphore, value)

        def steps(eng, phase_a, phase_b, between=None):
            for g in range(3):
                phase_a(g)
                if g == 0 and between:
                    between()
                phase_b(g)
            with eng.Fori(3, G) as g:
                phase_a(g)
                phase_b(g)
            for g in range(G, G + 2):
                phase_a(g)
                phase_b(g)

        def emptied(g, u):
            if u < 6:
                return live(g) and ((qk_set[0], g * 4 + u + 1) if u < 4 else (v_set[0], g * 2 + u - 3))
            if u in (11, 13):
                return live(g) and (sum_set[0], g * 2 + (u - 11) // 2 + 1)
            if u < 10:
                return live(g - 1) and (qk_set[1], (g - 1) * 4 + u - 5)
            return live(g - 1) and (v_set[1], (g - 1) * 2 + (1 if u == 10 else 2))

        def need_bank(eng, g, u):
            for back in range(2, 14, 2):
                s, n = (g, u - back) if u >= back else (g - 1, u - back + 14)
                if isinstance(s, int) and s < 0:
                    return
                last = emptied(s, n)
                if last:
                    eng.wait_ge(*last)
                    return

        block = ctx.enter_context(nc.Block())

        @block.sync
        def _(sp):
            sp.dma_start(xt_raw[:], x_feat[0]).then_inc(raw_in, 16)
            halves = [(n, half) for n in WEIGHTS for half in range(2)]
            for i, (n, half) in enumerate(halves):
                if i >= N_STAGE:
                    sp.wait_ge(w_hi_set, i - N_STAGE + 1)
                    sp.wait_ge(w_lo_set, i - N_STAGE + 1)
                sp.dma_start(stage[i % N_STAGE].rearrange("p (c n) -> p c n", c=2),
                             wts[n].rearrange("(c p) n -> p c n", p=P)[:, 2 * half:2 * half + 2, :]
                             ).then_inc(staged[i % N_STAGE], 16)
                if i == FIRST_W:
                    sp.dma_start(x_res[:], x_tok[0]).then_inc(x_in, 16)

            def phase_a(g):
                if live(g + 1) and not (isinstance(g, int) and g + 1 >= G):
                    load_raw(g + 1)
                if live(g) and not (isinstance(g, int) and g == 0):
                    need(sp, ln_set[0], g * 2)
                    sp.dma_start(x_res[:], x_tok[g]).then_inc(x_in, 16)
                if live(g - 2):
                    carry_blocks(1, g - 2, 0)
                    carry_blocks(1, g - 2, 1)
                    store(g - 2, 0)

            def carry_blocks(l, group, b):
                if l == 0 and live(group - 2):
                    sp.wait_ge(att_done[1], (group - 2) * 2 + b + 1)
                elif l == 1 and live(group + 1):
                    sp.wait_ge(att_done[0], (group + 1) * 2 + b + 1)
                else:
                    need(sp, att_done[l], group * 2 + b - 1)
                sp.sem_inc(sp_passed, 1)
                sp.wait_ge(blocks_set[l], group * 4 + 2 * b + 2)
                for n in range(BLK):
                    sp.dma_start(prob_t[b][:, n].rearrange("p e c q -> p (e c q)"),
                                 blocks_t[n * SQ:(n + 1) * SQ].rearrange("p n e c q -> p n (e c q)")
                                 ).then_inc(probt_in[l], 16)

            def load_raw(g):
                need(sp, x0_hi_set, g)
                need(sp, x0_lo_set, g)
                sp.dma_start(xt_raw[:], x_feat[g]).then_inc(raw_in, 16)

            def store(j, b):
                sp.wait_ge(ln_set[1], j * 2 + b + 1)
                sp.dma_start(out[j, b], y[:, b, :]).then_inc(y_out[b], 16)

            def phase_b(g):
                if live(g):
                    carry_blocks(0, g, 0)
                if live(g - 2):
                    store(g - 2, 1)
                if live(g):
                    carry_blocks(0, g, 1)

            for g in range(3):
                phase_a(g)
                phase_b(g)
            with sp.Fori(3, G - 1) as g:
                phase_a(g)
                phase_b(g)
            for g in range(G - 1, G + 2):
                phase_a(g)
                phase_b(g)
            for b in range(GB):
                sp.wait_ge(y_out[b], 16 * G)

        @block.tensor
        def _(pe):
            def project_t(l, ps_out, w, chunks, done):
                for i, m in enumerate(chunks):
                    cols = slice(m * P, m * P + P)
                    for c in range(NC):
                        parts = [(w_hi[w], xt_hi[l]), (w_hi[w], xt_lo[l]), (w_lo[w], xt_hi[l])]
                        for n, (wp, xp) in enumerate(parts):
                            last = pe.matmul(ps_out[:, i * T:(i + 1) * T], wp[:, c, cols], xp[:, c, :],
                                             start=(c == 0 and n == 0), stop=(c == NC - 1 and n == 2))
                last.then_inc(done, 1)

            def project(ps_out, hi, lo, w, done):
                for c in range(NC):
                    parts = [(hi(c), w_hi[w]), (hi(c), w_lo[w]), (lo(c), w_hi[w])]
                    for n, (xp, wp) in enumerate(parts):
                        last = pe.matmul(ps_out[:, :], xp, wp[:, c, :],
                                         start=(c == 0 and n == 0), stop=(c == NC - 1 and n == 2))
                last.then_inc(done, 1)

            def unit(l, g, u, group, i):
                need_bank(pe, g, u)
                bank = ps_proj[u % 2]
                if i < 4:
                    project_t(l, bank, ("q" if i < 2 else "k") + str(l), (2 * (i % 2), 2 * (i % 2) + 1), qk_done[l])
                else:
                    tok = slice((i - 4) * NODES, (i - 3) * NODES)
                    project(bank, lambda c: xt_hi[l][:, c, tok], lambda c: xt_lo[l][:, c, tok], f"v{l}", v_done[l])

            def scores(l, group, b, bank_free):
                tok = slice(b * NODES, (b + 1) * NODES)
                for e in range(2):
                    if bank_free:
                        need(pe, bank_free[0], bank_free[1] + e)
                    rows = slice(e * HD, (e + 1) * HD)
                    for c in range(NC):
                        last = pe.matmul(ps_score[e][:, c, :], q_t[l][rows, c, tok], k_t[l][rows, c, tok],
                                         start=True, stop=True)
                    last.then_inc(score_done[l], 1)

            def attend(l, group, b):
                pe.wait_ge(probt_in[l], (group * 2 + b + 1) * 16 * BLK)
                pe.wait_ge(v_set[l], group * 2 + b + 1)
                for c in range(NC):
                    for e in range(2):
                        h = 2 * c + e
                        last = pe.matmul(ps_att[e * HD:(e + 1) * HD, c * NODES:(c + 1) * NODES],
                                         v[l][:, b, h * HD:(h + 1) * HD], prob_t[b][:, :, e, c, :],
                                         start=True, stop=True)
                last.then_inc(att_done[l], 1)

            def transpose_back(j, b):
                pe.wait_ge(at1_set, j * 2 + b + 1)
                need(pe, sum_set[1], j * 2 + b)
                for c in range(NC):
                    last = pe.transpose(ps_back[:, c * P:(c + 1) * P], at1[:, c, :], ident[:])
                last.then_inc(back_done, 1)

            def transpose_x1(m, b):
                pe.wait_ge(ln_set[0], m * 2 + b + 1)
                need(pe, x1_hi_set, m * 2 + b)
                need(pe, x1_lo_set, m * 2 + b)
                for c in range(NC):
                    last = pe.transpose(ps_x1t[:, c, :], x1[:, b, c * P:(c + 1) * P], ident[:])
                last.then_inc(x1t_done, 1)

            def phase_a(g):
                j, m = g - 2, g - 1
                att, proj, xt = live(j), live(g), live(m)

                def layer0_unit(i):
                    if proj:
                        if i == 0:
                            pe.wait_ge(x0_hi_set, g + 1)
                            pe.wait_ge(x0_lo_set, g + 1)
                        if isinstance(g, int) and g == 0 and i % 2 == 0:
                            pe.wait_ge(w_hi_set, i + 2)
                            pe.wait_ge(w_lo_set, i + 2)
                        unit(0, g, i, g, i)

                if att:
                    pe.wait_ge(qk_set[1], j * 4 + 4)
                    scores(1, j, 0, (masked_set[0], g * 4 - 1) if live(m) else (masked_set[1], j * 4 - 1))
                layer0_unit(0)
                layer0_unit(1)
                if xt:
                    transpose_x1(m, 0)
                if att:
                    scores(1, j, 1, (masked_set[1], j * 4 + 1))
                layer0_unit(2)
                if xt:
                    transpose_x1(m, 1)
                layer0_unit(3)
                if att:
                    if live(m):
                        need(pe, at_hi_set, g * 2)
                        need(pe, at_lo_set, g * 2)
                    else:
                        need(pe, at1_set, j * 2)
                    attend(1, j, 0)
                layer0_unit(4)
                if att:
                    transpose_back(j, 0)
                layer0_unit(5)
                if att:
                    pe.wait_ge(at1_set, j * 2 + 1)
                    attend(1, j, 1)

            def phase_b(g):
                j, m = g - 2, g - 1
                att, proj = live(g), live(m)

                def layer1_unit(i):
                    if proj:
                        if i == 0:
                            pe.wait_ge(x1_hi_set, m * 2 + 2)
                            pe.wait_ge(x1_lo_set, m * 2 + 2)
                        unit(1, g, (6, 7, 8, 9, 10, 12)[i], m, i)

                def wo(b):
                    pe.wait_ge(at_hi_set, g * 2 + b + 1)
                    pe.wait_ge(at_lo_set, g * 2 + b + 1)
                    u = 11 + 2 * b
                    need_bank(pe, g, u)
                    project(ps_proj[u % 2], lambda c: at_hi[:, c, :], lambda c: at_lo[:, c, :], "o0", wo_done)

                if att:
                    pe.wait_ge(qk_set[0], g * 4 + 4)
                    scores(0, g, 0, (masked_set[1], j * 4 + 3) if live(j) else (masked_set[0], g * 4 - 1))
                if live(j):
                    transpose_back(j, 1)
                layer1_unit(0)
                layer1_unit(1)
                if att:
                    scores(0, g, 1, (masked_set[0], g * 4 + 1))
                layer1_unit(2)
                layer1_unit(3)
                if att:
                    if live(j):
                        pe.wait_ge(at1_set, j * 2 + 2)
                    else:
                        need(pe, at_hi_set, g * 2)
                        need(pe, at_lo_set, g * 2)
                    attend(0, g, 0)
                layer1_unit(4)
                if att:
                    wo(0)
                    attend(0, g, 1)
                layer1_unit(5)
                if att:
                    wo(1)

            def bias_product():
                pe.wait_ge(ident_set, 2)
                pe.wait_ge(bv_split, 2)
                pe.wait_ge(w_hi_set, 2 * len(WEIGHTS))
                pe.wait_ge(w_lo_set, 2 * len(WEIGHTS))
                project(ps_att, lambda c: at_hi[:, c, :], lambda c: at_lo[:, c, :], "o0", bv_wo_done)
                pe.wait_ge(bo_set, 1)

            steps(pe, phase_a, phase_b, bias_product)

        @block.scalar
        def _(act):
            small = [(bq_col[0], "bq0"), (bk_col[0], "bk0"), (bv0_col, "bv0"), (bq_col[1], "bq1"), (bk_col[1], "bk1")]
            for tile, n in small:
                act.dma_start(tile[:], biases[n + "_col"]).then_inc(small_in, 16)
            for tile, n in ((bo_row, "bo0"), (bv1_row, "bv1")):
                act.dma_start(tile[:], biases[n].rearrange("(a n) -> a n", a=1).to_broadcast([P, D])
                              ).then_inc(small_in, 16)
            for tile in mask:
                act.dma_start(tile[:], adj).then_inc(small_in, 16)
            halves = [(n, half) for n in WEIGHTS for half in range(2)]
            for i, (n, half) in enumerate(halves[:FIRST_W]):
                act.wait_ge(staged[i % N_STAGE], 16 * (i // N_STAGE + 1))
                act.activation(w_hi[n][:, 2 * half:2 * half + 2, :].rearrange("p c n -> p (c n)"),
                               stage[i % N_STAGE], ACT.Copy).then_inc(w_hi_set, 1)

            def qk_out(l, g, u, group, i, freed_by, times):
                act.wait_ge(qk_done[l], group * 4 + i + 1)
                need(act, freed_by, times)
                tile = q_t[l] if i < 2 else k_t[l]
                bias = bq_scaled[l] if i < 2 else bk_col[l]
                for n in range(2):
                    m = 2 * (i % 2) + n
                    dst, src = tile[:, m, :], ps_proj[u % 2][:, n * T:(n + 1) * T]
                    if i >= 2:
                        dst = dst.rearrange("p (b j n) -> p b n j", b=GB, n=SQ)
                        src = src.rearrange("p (b n j) -> p b n j", b=GB, j=BLK)
                    last = act.activation(dst, src, ACT.Identity,
                                          bias=bias[:, m:m + 1], scale=SCALE if i < 2 else 1.0)
                last.then_inc(qk_set[l], 1)

            def v_out(l, u, group, b):
                act.wait_ge(v_done[l], group * 2 + b + 1)
                need(act, att_done[l], group * 2)
                act.activation(v[l][:, b, :], ps_proj[u % 2][:, :], ACT.Copy).then_inc(v_set[l], 1)

            def exps(l, group, b):
                for e in range(2):
                    act.wait_ge(masked_set[l], group * 4 + 2 * b + e + 1)
                    for c in range(NC):
                        last = act.activation(prob[b][:, e, c, :], prob[b][:, e, c, :], ACT.Exp,
                                              bias=neg_max[l][b][:, e, c:c + 1], scale=-1.0,
                                              accum_out=row_sum[l][b][:, e, c:c + 1])
                    last.then_inc(exp_set[l], 1)

            def at1_copy(j, b):
                act.wait_ge(att_done[1], j * 2 + b + 1)
                need(act, back_done, j * 2 + b)
                act.activation(at1[:].rearrange("p c n -> p (c n)"), ps_att[:], ACT.Copy).then_inc(at1_set, 1)

            def phase_a(g):
                j, m = g - 2, g - 1
                att, proj, xt = live(j), live(g), live(m)

                def q_or_k(i):
                    if proj:
                        qk_out(0, g, i, g, i, score_done[0], g * 4)

                def x1_hi(b):
                    if xt:
                        act.wait_ge(x1t_done, m * 2 + b + 1)
                        need(act, qk_done[1], m * 4)
                        need(act, v_done[1], m * 2)
                        act.activation(xt_hi[1][:, :, b * NODES:(b + 1) * NODES], ps_x1t[:], ACT.Copy
                                       ).then_inc(x1_hi_set, 1)

                def at1_out(b):
                    if att:
                        at1_copy(j, b)

                if isinstance(g, int) and g == 0:
                    act.wait_ge(consts_set, 1)
                if att:
                    exps(1, j, 0)
                q_or_k(0)
                q_or_k(1)
                x1_hi(0)
                if att:
                    exps(1, j, 1)
                q_or_k(2)
                x1_hi(1)
                q_or_k(3)
                at1_out(0)
                if proj:
                    v_out(0, 4, g, 0)
                    v_out(0, 5, g, 1)

            def phase_b(g):
                j, m = g - 2, g - 1
                att, proj = live(g), live(m)

                def q_or_k(i):
                    if proj:
                        qk_out(1, g, 6 + i, m, i, score_done[1], m * 4)

                def at_high(b):
                    if att:
                        act.wait_ge(att_done[0], g * 2 + b + 1)
                        need(act, wo_done, g * 2 + b)
                        act.activation(at_hi[:].rearrange("p c n -> p (c n)"), ps_att[:], ACT.Copy
                                       ).then_inc(at_hi_set, 1)

                if live(j):
                    at1_copy(j, 1)
                if att:
                    exps(0, g, 0)
                q_or_k(0)
                q_or_k(1)
                if att:
                    exps(0, g, 1)
                q_or_k(2)
                q_or_k(3)
                at_high(0)
                if proj:
                    v_out(1, 10, m, 0)
                at_high(1)
                if proj:
                    v_out(1, 12, m, 1)

            steps(act, phase_a, phase_b)

        @block.vector
        def _(dve):
            halves = [(n, half) for n in WEIGHTS for half in range(2)]

            def weight_low(i):
                n, half = halves[i]
                hi = w_hi[n][:, 2 * half:2 * half + 2, :].rearrange("p c n -> p (c n)")
                if i >= FIRST_W:
                    dve.wait_ge(staged[i % N_STAGE], 16 * (i // N_STAGE + 1))
                    dve.tensor_copy(hi, stage[i % N_STAGE]).then_inc(w_hi_set, 1)
                dve.wait_ge(w_hi_set, i + 1)
                dve.tensor_tensor(w_lo[n][:, 2 * half:2 * half + 2, :].rearrange("p c n -> p (c n)"),
                                  stage[i % N_STAGE], hi.bitcast(F32), ALU.subtract).then_inc(w_lo_set, 1)

            def x0_high(group):
                dve.wait_ge(raw_in, (group + 1) * 16)
                dve.tensor_copy(xt_hi[0][:], xt_raw[:]).then_inc(x0_hi_set, 1)

            dve.wait_ge(small_in, 16 * 9)
            for l in range(2):
                dve.tensor_scalar(bq_scaled[l][:], bq_col[l][:], SCALE, None, ALU.mult)
            dve.tensor_scalar(mask[0][:], mask[0][:], -1.0, 1.0, ALU.mult, ALU.add).then_inc(mask_step, 1)
            dve.wait_ge(mask_step, 1)
            dve.tensor_scalar(mask[0][:], mask[0][:], MASKED, None, ALU.mult).then_inc(mask_step, 1)
            dve.tensor_scalar(mask[1][:], mask[1][:], 0.0, MASKED, ALU.is_equal, ALU.mult).then_inc(mask_step, 1)
            dve.wait_ge(mask_step, 3)
            dve.tensor_copy(at_hi[:], bv0_col[:].unsqueeze(2).to_broadcast([P, NC, NODES])).then_inc(bv_split, 1)
            dve.wait_ge(bv_split, 1)
            dve.tensor_tensor(at_lo[:], bv0_col[:].unsqueeze(2).to_broadcast([P, NC, NODES]),
                              at_hi[:].bitcast(F32), ALU.subtract).then_inc(bv_split, 1)
            dve.memset(minus_half[:], -0.5).then_inc(consts_set, 1)
            x0_high(0)
            for i in range(FIRST_W):
                weight_low(i)

            def mask_scores(l, group, b):
                if l == 0 and live(group - 2):
                    need(dve, blocks_set[1], (group - 2) * 4 + 2 * b + 2)
                elif l == 1 and live(group + 1):
                    need(dve, blocks_set[0], (group + 1) * 4 + 2 * b + 2)
                else:
                    need(dve, blocks_set[l], group * 4 + 2 * b - 2)
                for e in range(2):
                    dve.wait_ge(score_done[l], group * 4 + 2 * b + e + 1)
                    dve.sem_inc(dve_passed, 1)
                    for c in range(NC):
                        last = dve.tensor_tensor_reduce(prob[b][:, e, c, :], ps_score[e][:, c, :], mask[l][:],
                                                        -1.0, BIG, ALU.add, ALU.min,
                                                        neg_max[l][b][:, e, c:c + 1])
                    last.then_inc(masked_set[l], 1)

            def invert_sums(l, group, b):
                for e in range(2):
                    dve.wait_ge(exp_set[l], group * 4 + 2 * b + e + 1)
                    dve.reciprocal(inv_sum[l][b][:, e, :], row_sum[l][b][:, e, :]).then_inc(inv_set[l], 1)

            def statistics(l, group, b):
                done = group * 2 + b + 1
                row = (x_res if l == 0 else y)[:, b, :]
                dve.wait_ge(sum_set[l], done)
                dve.bn_stats(stats[l][:, b, :], row).then_inc(stats_set[l], 1)
                dve.wait_ge(stats_set[l], done)
                dve.sem_inc(dve_passed, 1)
                dve.bn_aggr(mean_var[l][:, b, :], stats[l][:, b, :]).then_inc(mean_set[l], 1)
                dve.wait_ge(mean_set[l], done)
                dve.tensor_scalar(var_eps[l][:, b:b + 1], mean_var[l][:, b, 1:2], EPS, None, ALU.add
                                  ).then_inc(eps_set[l], 1)

            def normalise(l, group, b):
                done = group * 2 + b + 1
                dve.wait_ge(rstd_set[l], done)
                if l == 0:
                    need(dve, x1t_done, done - 2)
                    need(dve, x1_res_set, done - 2)
                src, dst = (x_res, x1) if l == 0 else (y, y)
                dve.tensor_scalar(dst[:, b, :], src[:, b, :], mean_var[l][:, b, 0:1], rstd[l][:, b:b + 1],
                                  ALU.subtract, ALU.mult).then_inc(ln_set[l], 1)

            def transpose_blocks(l, group, b, carried, times):
                need(dve, carried, times)
                for e in range(2):
                    dve.wait_ge(norm_set[l], group * 4 + 2 * b + e + 1)
                    dve.transpose(blocks_t[:, :, e].rearrange("p n c q -> p c n q"),
                                  prob[b][:, e].rearrange("p c (n k) -> p c n k", k=SQ)).then_inc(blocks_set[l], 1)

            def x1_low(m, b):
                dve.wait_ge(x1_hi_set, m * 2 + b + 1)
                tok = slice(b * NODES, (b + 1) * NODES)
                dve.tensor_tensor(xt_lo[1][:, :, tok], ps_x1t[:], xt_hi[1][:, :, tok].bitcast(F32), ALU.subtract
                                  ).then_inc(x1_lo_set, 1)

            def residual1(j, b):
                dve.wait_ge(back_done, j * 2 + b + 1)
                if not isinstance(j, int) or j > 0:
                    dve.wait_ge(y_out[b], j * 16)
                dve.wait_ge(x1_res_set, j * 2 + b + 1)
                dve.tensor_tensor(y[:, b, :], ps_back[:], x1_res[:, b, :], ALU.add).then_inc(sum_set[1], 1)

            def at_low(g, b):
                dve.wait_ge(at_hi_set, g * 2 + b + 1)
                dve.tensor_tensor(at_lo[:].rearrange("p c n -> p (c n)"), ps_att[:],
                                  at_hi[:].rearrange("p c n -> p (c n)").bitcast(F32), ALU.subtract
                                  ).then_inc(at_lo_set, 1)

            def residual0(g, b):
                dve.wait_ge(wo_done, g * 2 + b + 1)
                dve.wait_ge(x_res_set, g + 1)
                dve.tensor_tensor(x_res[:, b, :], ps_proj[1][:, :], x_res[:, b, :], ALU.add).then_inc(sum_set[0], 1)

            def phase_a(g):
                j, m = g - 2, g - 1
                per = 2 * 16 * BLK
                if live(j):
                    mask_scores(1, j, 0)
                    invert_sums(1, j, 0)
                if live(m):
                    normalise(0, m, 1)
                if live(j):
                    transpose_blocks(1, j, 0, *((probt_in[0], g * per) if live(m) else (probt_in[1], j * per)))
                if live(m):
                    x1_low(m, 0)
                if live(j):
                    mask_scores(1, j, 1)
                    invert_sums(1, j, 1)
                if live(m):
                    x1_low(m, 1)
                if live(j):
                    transpose_blocks(1, j, 1, probt_in[1], j * per + per // 2)
                    residual1(j, 0)
                    statistics(1, j, 0)
                    normalise(1, j, 0)

            def phase_b(g):
                j = g - 2
                per = 2 * 16 * BLK
                att = live(g)
                if att:
                    mask_scores(0, g, 0)
                    invert_sums(0, g, 0)
                if live(j):
                    residual1(j, 1)
                    statistics(1, j, 1)
                if att:
                    transpose_blocks(0, g, 0, *((probt_in[1], j * per + per) if live(j) else (probt_in[0], g * per)))
                    if not isinstance(g, int) or g + 1 < G:
                        dve.wait_ge(qk_done[0], g * 4 + 4)
                        dve.wait_ge(v_done[0], g * 2 + 2)
                        x0_high(g + 1)
                if live(j):
                    normalise(1, j, 1)
                if att:
                    mask_scores(0, g, 1)
                    invert_sums(0, g, 1)
                    transpose_blocks(0, g, 1, probt_in[0], g * per + per // 2)
                    at_low(g, 0)
                    residual0(g, 0)
                    at_low(g, 1)
                    statistics(0, g, 0)
                    normalise(0, g, 0)
                    residual0(g, 1)
                    statistics(0, g, 1)

            def other_weights():
                for i in range(FIRST_W, len(halves)):
                    weight_low(i)
                dve.wait_ge(bv_wo_done, 1)
                dve.tensor_tensor(bo_row[:], ps_att[:], bo_row[:], ALU.add).then_inc(bo_set, 1)

            for g in range(3):
                phase_a(g)
                if g == 0:
                    other_weights()
                phase_b(g)
            with dve.Fori(3, G - 1) as g:
                phase_a(g)
                phase_b(g)
            for g in range(G - 1, G + 2):
                phase_a(g)
                phase_b(g)

        @block.gpsimd
        def _(pool):
            pool.memset(ident[:], 0.0).then_inc(ident_set, 1)
            pool.wait_ge(ident_set, 1)
            pool.affine_select(out=ident[:], in_=ident[:], compare_op=ALU.not_equal, fill=1.0, base=0,
                               pattern=[[-1, P]], channel_multiplier=1).then_inc(ident_set, 1)

            def x0_low(group):
                pool.wait_ge(x0_hi_set, group + 1)
                pool.tensor_tensor(xt_lo[0][:], xt_raw[:], xt_hi[0][:].bitcast(F32), ALU.subtract
                                   ).then_inc(x0_lo_set, 1)

            def inverse_deviation(l, group, b):
                done = group * 2 + b + 1
                pool.wait_ge(eps_set[l], done)
                need(pool, ln_set[l], done - 2)
                pool.tensor_tensor(rstd[l][:, b:b + 1], var_eps[l][:, b:b + 1], minus_half[:], ALU.pow
                                   ).then_inc(rstd_set[l], 1)

            def normalise_probs(l, group, b):
                for e in range(2):
                    pool.wait_ge(inv_set[l], group * 4 + 2 * b + e + 1)
                    pool.tensor_tensor(prob[b][:, e], prob[b][:, e],
                                       inv_sum[l][b][:, e, :].unsqueeze(2).to_broadcast([P, NC, NODES]), ALU.mult
                                       ).then_inc(norm_set[l], 1)

            def copy_x1(m, b):
                pool.wait_ge(ln_set[0], m * 2 + b + 1)
                need(pool, sum_set[1], m * 2 + b - 1)
                pool.tensor_tensor(x1_res[:, b, :], x1[:, b, :], bv1_row[:], ALU.add).then_inc(x1_res_set, 1)

            def phase_a(g):
                j, m = g - 2, g - 1
                if live(m):
                    inverse_deviation(0, m, 1)
                if live(j):
                    normalise_probs(1, j, 0)
                if live(j):
                    normalise_probs(1, j, 1)
                if live(g):
                    pool.wait_ge(x_in, (g + 1) * 16)
                    if isinstance(g, int) and g == 0:
                        pool.wait_ge(bo_set, 1)
                    pool.tensor_tensor(x_res[:], x_res[:], bo_row[:].unsqueeze(1).to_broadcast([P, GB, D]), ALU.add
                                       ).then_inc(x_res_set, 1)
                if live(j):
                    inverse_deviation(1, j, 0)

            def phase_b(g):
                j, m = g - 2, g - 1
                if live(g):
                    normalise_probs(0, g, 0)
                if live(j):
                    inverse_deviation(1, j, 1)
                if live(m):
                    copy_x1(m, 0)
                    copy_x1(m, 1)
                if live(g):
                    normalise_probs(0, g, 1)
                    if not isinstance(g, int) or g + 1 < G:
                        x0_low(g + 1)
                    inverse_deviation(0, g, 0)

            pool.wait_ge(consts_set, 1)
            x0_low(0)
            for g in range(3):
                phase_a(g)
                phase_b(g)
            with pool.Fori(3, G - 1) as g:
                phase_a(g)
                phase_b(g)
            for g in range(G - 1, G + 2):
                phase_a(g)
                phase_b(g)


def kernel(**inputs):
    import numpy as np
    import concourse.bacc as bacc
    from concourse.bass_utils import run_bass_kernel_spmd

    nc = bacc.Bacc("TRN2", target_bir_lowering=False, num_devices=1)
    x = np.asarray(inputs["x"])
    graphs = x.shape[0]
    groups = graphs // GB
    arrays = {
        "x_tok": np.ascontiguousarray(x.reshape(groups, GB, NODES, D).transpose(0, 2, 1, 3)),
        "x_feat": np.ascontiguousarray(x.reshape(groups, T, NC, P).transpose(0, 3, 2, 1)),
        "adj": np.ascontiguousarray(
            np.asarray(inputs["adj"]).reshape(NODES, SQ, BLK).transpose(0, 2, 1).reshape(NODES, NODES)),
    }
    names = {"q0": "L0_gnn_Wq", "k0": "L0_gnn_Wk", "v0": "L0_gnn_Wv", "o0": "L0_gnn_Wo",
             "q1": "L1_gnn_Wq", "k1": "L1_gnn_Wk", "v1": "L1_gnn_Wv"}
    for short, name in names.items():
        arrays[f"w_{short}"] = np.ascontiguousarray(inputs[name])
        bias = np.asarray(inputs[name.replace("_W", "_b")])
        arrays[f"b_{short}"] = np.ascontiguousarray(bias)
        arrays[f"b_{short}_col"] = np.ascontiguousarray(bias.reshape(NC, P).T)
    aps = {n: nc.dram_tensor(n, a.shape, mybir.dt.from_np(a.dtype), kind="ExternalInput").ap()
           for n, a in arrays.items()}
    out = nc.dram_tensor("out", (groups, GB, NODES, D), F32, kind="ExternalOutput").ap()
    adj_resnorm_kernel(nc, aps["x_tok"], aps["x_feat"], aps["adj"], {s: aps[f"w_{s}"] for s in names},
                       {n.replace("b_", "b"): ap for n, ap in aps.items() if n.startswith("b_")}, out)
    result = run_bass_kernel_spmd(nc, [arrays], core_ids=[0])
    return result.results[0]["out"].reshape(graphs, NODES, D)
```

```python
from contextlib import ExitStack

import concourse.bass as bass
from concourse import mybir

F32 = mybir.dt.float32
F32R = mybir.dt.float32r
ALU = mybir.AluOpType
ACT = mybir.ActivationFunctionType

P = 128
NODES = 128
D = 512
H = 8
HD = D // H
HB = 4
HALVES = H // HB
NC = D // P
GB = 2
T = GB * NODES
SCALE = 1.0 / 8.0
EPS = 1e-5
SQ = 32
BLK = P // SQ
MASKED = -1000000000.0
BIG = 3.0e38
WEIGHTS = ["q0", "k0", "v0", "o0", "q1", "k1", "v1"]
N_STAGE = 6
DVE_W = 2
FIRST_W = 6

assert HD * 2 == P and NC * 2 == H and HB == NC


def adj_resnorm_kernel(nc, x_tok, x_feat, adj, wts, biases, out):
    G = x_feat.shape[0]

    def live(group):
        return not isinstance(group, int) or 0 <= group < G

    with ExitStack() as ctx:
        def sb(name, shape, dt=F32):
            return ctx.enter_context(nc.sbuf_tensor(name, shape, dt))

        def ps(name, shape):
            return ctx.enter_context(nc.psum_tensor(name, shape, F32))

        def sem(name):
            return ctx.enter_context(nc.semaphore(name))

        w_hi = {n: sb(f"w_hi_{n}", [P, NC, D], F32R) for n in WEIGHTS}
        w_lo = {n: sb(f"w_lo_{n}", [P, NC, D], F32R) for n in WEIGHTS}
        xt_hi = [sb(f"xt_hi{l}", [P, NC, T], F32R) for l in range(2)]
        xt_lo = [sb(f"xt_lo{l}", [P, NC, T], F32R) for l in range(2)]
        q_hi, q_lo = sb("q_hi", [P, NC, T], F32R), sb("q_lo", [P, NC, T], F32R)
        k_hi, k_lo = (sb(n, [P, GB, NC, 2, NODES], F32R) for n in ("k_hi", "k_lo"))
        k_raw = sb("k_raw", [P, 2, T])
        v_first = sb("v_first", [P, D])
        v = [[v_first, sb(f"v_second{l}", [P, D])] for l in range(2)]
        x_res = sb("x_res", [P, GB, D])
        x1 = sb("x1", [P, GB, D])
        x1_res = sb("x1_res", [P, GB, D])
        prob = [sb(f"prob{b}", [P, HALVES, HB, NODES]) for b in range(GB)]
        blocks_t = sb("blocks_t", [P, BLK, HALVES, HB, SQ])
        prob_t = [sb(f"prob_t{b}", [P, BLK, HALVES, HB, SQ]) for b in range(GB)]
        at_hi = sb("at_hi", [P, NC, NODES], F32R)
        at_lo = sb("at_lo", [P, NC, NODES], F32R)
        y = sb("y", [P, GB, D])
        x1_blocks = [blocks_t[:].rearrange("p n i h q -> p (n i h q)")[:, :D], y[:, 0, :]]
        x1_turned = [place.rearrange("p (n c t) -> p n c t", n=BLK, c=NC)
                     for place in (prob_t[1][:].rearrange("p n i h q -> p (n i h q)")[:, :D], y[:, 1, :])]
        xt_raw = y[:].rearrange("p b (c n) -> p (b c) n", n=T)
        prob_flat = [s[:].rearrange("p i h n -> p (i h n)") for s in prob]
        at1 = [s[:, :D].rearrange("p (c n q) -> p c n q", n=BLK, q=SQ) for s in prob_flat]
        at1_blocks = [s[:, D:] for s in prob_flat]
        at1_turned = [s[:].rearrange("p n i h q -> p (n i h q)")[:, :D].rearrange("p (r c f) -> p r c f", r=BLK, c=NC)
                      for s in prob_t]
        mask = [sb(f"mask{l}", [P, NODES]) for l in range(2)]
        bo_row = sb("bo_row", [P, D])
        bv1_row = sb("bv1_row", [P, D])
        bq_col = [sb(f"bq_col{l}", [P, NC]) for l in range(2)]
        bk_col = [sb(f"bk_col{l}", [P, NC]) for l in range(2)]
        bv0_col = sb("bv0_col", [P, NC])
        neg_max = [[sb(f"neg_max{l}{b}", [P, HALVES, HB]) for b in range(GB)] for l in range(2)]
        row_sum = [[sb(f"row_sum{l}{b}", [P, HALVES, HB]) for b in range(GB)] for l in range(2)]
        inv_sum = [[sb(f"inv_sum{l}{b}", [P, HALVES, HB]) for b in range(GB)] for l in range(2)]
        stats = [sb(f"stats{l}", [P, GB, 6]) for l in range(2)]
        mean_var = [sb(f"mean_var{l}", [P, GB, 2]) for l in range(2)]
        var_eps = [sb(f"var_eps{l}", [P, GB]) for l in range(2)]
        rstd = [sb(f"rstd{l}", [P, GB]) for l in range(2)]
        minus_half = sb("minus_half", [P, 1])

        stage = [s[:].rearrange("p a b c -> p (a b c)") for s in prob] + \
                [s[:].rearrange("p a b c d -> p (a b c d)") for s in (*prob_t, blocks_t)] + \
                [x1_res[:].rearrange("p b n -> p (b n)")]

        ps_proj = [ps(f"ps_proj{i}", [P, 512]) for i in range(2)]
        ps_score = [[ps(f"ps_score{b}{i}", [P, HB, NODES]) for i in range(HALVES)] for b in range(GB)]
        ps_att = ps("ps_att", [P, 512])

        staged = [sem(f"staged{i}") for i in range(N_STAGE)]
        w_hi_set = sem("w_hi_set")
        w_lo_set = sem("w_lo_set")
        small_in = sem("small_in")
        consts_set = sem("consts_set")
        dve_passed = sem("dve_passed")
        sp_passed = sem("sp_passed")
        mask_step = sem("mask_step")
        bv_split = sem("bv_split")
        bv_wo_done = sem("bv_wo_done")
        bo_set = sem("bo_set")
        zeros_set = sem("zeros_set")
        raw_in = [sem(f"raw_in{half}") for half in range(2)]
        x_in = sem("x_in")
        y_out = [sem(f"y_out{b}") for b in range(GB)]
        x0_hi_set = sem("x0_hi_set")
        x0_lo_set = sem("x0_lo_set")
        x_res_set = sem("x_res_set")
        qk_done = [sem(f"qk_done{l}") for l in range(2)]
        q_hi_set = [sem(f"q_hi_set{l}") for l in range(2)]
        q_lo_set = [sem(f"q_lo_set{l}") for l in range(2)]
        k_raw_set = [sem(f"k_raw_set{l}") for l in range(2)]
        k_hi_set = [sem(f"k_hi_set{l}") for l in range(2)]
        k_lo_even_set = [sem(f"k_lo_even_set{l}") for l in range(2)]
        k_lo_odd_set = [sem(f"k_lo_odd_set{l}") for l in range(2)]
        v_done = [sem(f"v_done{l}") for l in range(2)]
        v_set = [sem(f"v_set{l}") for l in range(2)]
        score_done = [sem(f"score_done{l}") for l in range(2)]
        masked_set = [sem(f"masked_set{l}") for l in range(2)]
        exp_set = [sem(f"exp_set{l}") for l in range(2)]
        inv_set = [sem(f"inv_set{l}") for l in range(2)]
        norm_set = [sem(f"norm_set{l}") for l in range(2)]
        blocks_set = [sem(f"blocks_set{l}") for l in range(2)]
        probt_in = [sem(f"probt_in{l}") for l in range(2)]
        att_done = [sem(f"att_done{l}") for l in range(2)]
        at_hi_set = sem("at_hi_set")
        at_lo_set = sem("at_lo_set")
        wo_done = sem("wo_done")
        at1_set = sem("at1_set")
        at1_blocks_set = sem("at1_blocks_set")
        at1_in = [sem(f"at1_in{b}") for b in range(GB)]
        sum_set = [sem(f"sum_set{l}") for l in range(2)]
        stats_set = [sem(f"stats_set{l}") for l in range(2)]
        mean_set = [sem(f"mean_set{l}") for l in range(2)]
        eps_set = [sem(f"eps_set{l}") for l in range(2)]
        rstd_set = [sem(f"rstd_set{l}") for l in range(2)]
        ln_set = [sem(f"ln_set{l}") for l in range(2)]
        x1_blocks_set = sem("x1_blocks_set")
        x1t_in = [sem(f"x1t_in{b}") for b in range(GB)]
        x1_hi_set = sem("x1_hi_set")
        x1_lo_set = sem("x1_lo_set")
        x1_res_set = sem("x1_res_set")

        def need(eng, semaphore, value):
            if not isinstance(value, int) or value > 0:
                eng.wait_ge(semaphore, value)

        def steps(eng, phase_a, phase_b, last_steps, between=None):
            for g in range(3):
                phase_a(g)
                if g == 0 and between:
                    between()
                phase_b(g)
            with eng.Fori(3, G) as g:
                phase_a(g)
                phase_b(g)
            last_steps()

        def emptied(g, u):
            def of_layer(l, group, i):
                if i < 4:
                    return (q_lo_set if i < 2 else k_raw_set)[l], group * 2 + i % 2 + 1
                return v_set[l], group * 2 + i - 3
            if u < 6:
                return live(g) and of_layer(0, g, u)
            if u >= 12:
                return live(g) and (sum_set[0], g * 2 + u - 11)
            return live(g - 1) and of_layer(1, g - 1, u - 6)

        def need_bank(eng, g, u):
            for back in range(2, 14, 2):
                s, n = (g, u - back) if u >= back else (g - 1, u - back + 14)
                if isinstance(s, int) and s < 0:
                    return
                last = emptied(s, n)
                if last:
                    eng.wait_ge(*last)
                    return

        def k_block(part, i, e):
            return part[e * HD:(e + 1) * HD, :, 2 * i:2 * i + 2, e, :]

        def k_source(e):
            return k_raw[e * HD:(e + 1) * HD].rearrange("p c (b n) -> p b c n", b=GB)

        def x0_half(part, half):
            return part[:, half * NC // 2:(half + 1) * NC // 2, :]

        def x1_part(part, b):
            return part[1][:, :, b * NODES:(b + 1) * NODES].rearrange("p c (n t) -> p c n t", n=BLK)

        block = ctx.enter_context(nc.Block())

        @block.sync
        def _(sp):
            for half in range(2):
                sp.dma_start(x0_half(xt_raw, half), x0_half(x_feat[0], half)).then_inc(raw_in[half], 16)
            halves = [(n, half) for n in WEIGHTS for half in range(2)]
            for i, (n, half) in enumerate(halves):
                if i >= N_STAGE:
                    sp.wait_ge(w_hi_set, i - N_STAGE + 1)
                    sp.wait_ge(w_lo_set, i - N_STAGE + 1)
                sp.dma_start(stage[i % N_STAGE].rearrange("p (c n) -> p c n", c=2),
                             wts[n].rearrange("(c p) n -> p c n", p=P)[:, 2 * half:2 * half + 2, :]
                             ).then_inc(staged[i % N_STAGE], 16)
                if i == FIRST_W + 1:
                    sp.dma_start(x_res[:], x_tok[0]).then_inc(x_in, 16)

            def phase_a(g):
                if live(g - 1):
                    carry_x1(g - 1, 0)
                if live(g - 2):
                    carry_blocks(1, g - 2, 0)
                if live(g - 1):
                    carry_x1(g - 1, 1)
                if live(g) and not (isinstance(g, int) and g == 0):
                    need(sp, ln_set[0], g * 2)
                    sp.dma_start(x_res[:], x_tok[g]).then_inc(x_in, 16)
                if live(g - 2):
                    carry_blocks(1, g - 2, 1)
                    carry_at1(g - 2, 0)

            def carry_blocks(l, group, b):
                if l == 0 and live(group - 2):
                    sp.wait_ge(att_done[1], (group - 2) * 2 + b + 1)
                elif l == 1 and live(group + 1):
                    sp.wait_ge(att_done[0], (group + 1) * 2 + b + 1)
                else:
                    need(sp, att_done[l], group * 2 + b - 1)
                if l == 0 and live(group - 2):
                    sp.sem_inc(sp_passed, 1)
                    sp.wait_ge(sum_set[1], (group - 2) * 2 + b + 1)
                elif l == 1 and not live(group + 1):
                    need(sp, sum_set[1], group * 2 + b - 1)
                sp.sem_inc(sp_passed, 1)
                m = group + 1 if l == 1 else group - 1
                if b == 1 and live(m) and (l == 1 or not live(group - 2)):
                    sp.wait_ge(x1_hi_set, m * 2 + 1)
                    sp.sem_inc(sp_passed, 1)
                    sp.wait_ge(x1_lo_set, m * 2 + 1)
                    sp.sem_inc(sp_passed, 1)
                sp.wait_ge(blocks_set[l], group * 4 + 2 * b + 2)
                for n in range(BLK):
                    sp.dma_start(prob_t[b][:, n].rearrange("p e c q -> p (e c q)"),
                                 blocks_t[n * SQ:(n + 1) * SQ].rearrange("p n e c q -> p n (e c q)")
                                 ).then_inc(probt_in[l], 16)

            def carry_at1(j, b):
                sp.wait_ge(att_done[1], j * 2 + b + 1)
                sp.sem_inc(sp_passed, 1)
                sp.wait_ge(at1_blocks_set, j * 2 + b + 1)
                for n in range(BLK):
                    sp.dma_start(at1_turned[b][:, n].rearrange("p c f -> p (c f)"),
                                 at1_blocks[b][n * SQ:(n + 1) * SQ].rearrange("p (n k) -> p n k", n=BLK)
                                 ).then_inc(at1_in[b], 16)

            def carry_x1(m, b):
                if b == 0:
                    sp.wait_ge(att_done[0], m * 2 + 2)
                    sp.sem_inc(sp_passed, 1)
                sp.wait_ge(x1_blocks_set, m * 2 + b + 1)
                for n in range(BLK):
                    sp.dma_start(x1_turned[b][:, n].rearrange("p c t -> p (c t)"),
                                 x1_blocks[b][n * SQ:(n + 1) * SQ].rearrange("p (n k) -> p n k", n=BLK)
                                 ).then_inc(x1t_in[b], 16)

            def load_raw(g, half):
                need(sp, x0_hi_set, g * 2)
                need(sp, x0_lo_set, g * 2)
                sp.sem_inc(sp_passed, 1)
                if live(g - 2):
                    sp.wait_ge(x1_hi_set, (g - 1) * 2)
                    sp.sem_inc(sp_passed, 1)
                    sp.wait_ge(x1_lo_set, (g - 1) * 2)
                    sp.sem_inc(sp_passed, 1)
                if live(g - 3):
                    sp.wait_ge(y_out[half], (g - 2) * 16)
                    sp.sem_inc(sp_passed, 1)
                sp.dma_start(x0_half(xt_raw, half), x0_half(x_feat[g], half)).then_inc(raw_in[half], 16)

            def store(j, b):
                sp.wait_ge(ln_set[1], j * 2 + b + 1)
                sp.dma_start(out[j, b], y[:, b, :]).then_inc(y_out[b], 16)

            def phase_b(g):
                y_unused = not live(g - 2)
                if y_unused and live(g + 1):
                    load_raw(g + 1, 0)
                    load_raw(g + 1, 1)
                if live(g - 2):
                    carry_at1(g - 2, 1)
                if live(g):
                    carry_blocks(0, g, 0)
                if live(g - 2):
                    store(g - 2, 0)
                if not y_unused and live(g + 1):
                    load_raw(g + 1, 0)
                if live(g):
                    carry_blocks(0, g, 1)
                if live(g - 2):
                    store(g - 2, 1)
                if not y_unused and live(g + 1):
                    load_raw(g + 1, 1)

            def last_steps():
                carry_x1(G - 1, 0)
                carry_x1(G - 1, 1)
                carry_blocks(1, G - 2, 0)
                carry_blocks(1, G - 2, 1)
                carry_at1(G - 2, 0)
                carry_at1(G - 2, 1)
                store(G - 2, 0)
                carry_blocks(1, G - 1, 0)
                store(G - 2, 1)
                carry_blocks(1, G - 1, 1)
                carry_at1(G - 1, 0)
                carry_at1(G - 1, 1)
                store(G - 1, 0)
                store(G - 1, 1)

            for g in range(3):
                phase_a(g)
                phase_b(g)
            with sp.Fori(3, G - 1) as g:
                phase_a(g)
                phase_b(g)
            phase_a(G - 1)
            phase_b(G - 1)
            last_steps()
            for b in range(GB):
                sp.wait_ge(y_out[b], 16 * G)

        @block.tensor
        def _(pe):
            def project_t(l, ps_out, w, chunks, done):
                for i, m in enumerate(chunks):
                    cols = slice(m * P, m * P + P)
                    for c in range(NC):
                        parts = [(w_hi[w], xt_hi[l]), (w_hi[w], xt_lo[l]), (w_lo[w], xt_hi[l])]
                        for n, (wp, xp) in enumerate(parts):
                            last = pe.matmul(ps_out[:, i * T:(i + 1) * T], wp[:, c, cols], xp[:, c, :],
                                             start=(c == 0 and n == 0), stop=(c == NC - 1 and n == 2))
                last.then_inc(done, 1)

            def project(ps_out, hi, lo, w, done):
                for c in range(NC):
                    parts = [(hi(c), w_hi[w]), (hi(c), w_lo[w]), (lo(c), w_hi[w])]
                    for n, (xp, wp) in enumerate(parts):
                        last = pe.matmul(ps_out[:, :], xp, wp[:, c, :],
                                         start=(c == 0 and n == 0), stop=(c == NC - 1 and n == 2))
                last.then_inc(done, 1)

            def unit(l, g, u, group, i):
                need_bank(pe, g, u)
                bank = ps_proj[u % 2]
                if i < 4:
                    project_t(l, bank, ("q" if i < 2 else "k") + str(l), (2 * (i % 2), 2 * (i % 2) + 1), qk_done[l])
                else:
                    tok = slice((i - 4) * NODES, (i - 3) * NODES)
                    project(bank, lambda c: xt_hi[l][:, c, tok], lambda c: xt_lo[l][:, c, tok], f"v{l}", v_done[l])

            def scores(l, group, b, banks_free, count):
                pe.wait_ge(q_lo_set[l], group * 2 + 2)
                pe.wait_ge(k_lo_even_set[l], group * 2 + 2)
                pe.wait_ge(k_lo_odd_set[l], group * 2 + 2)
                tok = slice(b * NODES, (b + 1) * NODES)
                for i in range(HALVES):
                    need(pe, banks_free, count + 2 * b + i + 1)
                    for c in (2 * i, 2 * i + 1):
                        ps_pair = ps_score[b][i][:, 2 * (c % 2):2 * (c % 2) + 2, :]
                        parts = [(q_hi, k_hi), (q_hi, k_lo), (q_lo, k_hi)]
                        for n, (qp, kp) in enumerate(parts):
                            last = pe.matmul(ps_pair, qp[:, c, tok], kp[:, b, c], start=(n == 0), stop=(n == 2))
                    last.then_inc(score_done[l], 1)

            def attend(l, group, b):
                pe.wait_ge(probt_in[l], (group * 2 + b + 1) * 16 * BLK)
                pe.wait_ge(v_set[l], group * 2 + b + 1)
                for c in range(NC):
                    for e in range(2):
                        h = 2 * c + e
                        last = pe.matmul(ps_att[e * HD:(e + 1) * HD, c * NODES:(c + 1) * NODES],
                                         v[l][b][:, h * HD:(h + 1) * HD], prob_t[b][:, :, h // HB, h % HB, :],
                                         start=True, stop=True)
                last.then_inc(att_done[l], 1)

            def wo(group, b):
                pe.wait_ge(at_hi_set, group * 2 + b + 1)
                pe.wait_ge(at_lo_set, group * 2 + b + 1)
                need_bank(pe, group, 12 + b)
                project(ps_proj[b], lambda c: at_hi[:, c, :], lambda c: at_lo[:, c, :], "o0", wo_done)

            def phase_a(g):
                j, m = g - 2, g - 1
                att, proj = live(j), live(g)

                def layer0_unit(i):
                    if proj:
                        if i == 0:
                            pe.wait_ge(x0_hi_set, g * 2 + 2)
                            pe.wait_ge(x0_lo_set, g * 2 + 2)
                        if isinstance(g, int) and g == 0 and i % 2 == 0:
                            pe.wait_ge(w_hi_set, i + 2)
                            pe.wait_ge(w_lo_set, i + 2)
                        unit(0, g, i, g, i)

                if att:
                    free = (masked_set[0], m * 4) if live(m) else (masked_set[1], j * 4 - 4)
                    scores(1, j, 0, *free)
                    scores(1, j, 1, *free)
                if live(m):
                    wo(m, 1)
                layer0_unit(0)
                layer0_unit(1)
                layer0_unit(2)
                layer0_unit(3)
                if att:
                    if live(m):
                        need(pe, at_hi_set, g * 2)
                        need(pe, at_lo_set, g * 2)
                    else:
                        need(pe, at1_set, j * 2)
                    attend(1, j, 0)
                layer0_unit(4)
                layer0_unit(5)
                if att:
                    pe.wait_ge(at1_set, j * 2 + 1)
                    attend(1, j, 1)

            def phase_b(g):
                j, m = g - 2, g - 1
                att, proj = live(g), live(m)

                def layer1_unit(i):
                    if proj:
                        if i == 0:
                            pe.wait_ge(x1_hi_set, m * 2 + 2)
                            pe.wait_ge(x1_lo_set, m * 2 + 2)
                        if isinstance(g, int) and g == 1 and i == 0:
                            pe.wait_ge(w_hi_set, 2 * len(WEIGHTS))
                            pe.wait_ge(w_lo_set, 2 * len(WEIGHTS))
                        unit(1, g, 6 + i, m, i)

                if att:
                    free = (masked_set[1], j * 4) if live(j) else (masked_set[0], g * 4 - 4)
                    scores(0, g, 0, *free)
                    scores(0, g, 1, *free)
                layer1_unit(0)
                layer1_unit(1)
                layer1_unit(2)
                layer1_unit(3)
                layer1_unit(4)
                if att:
                    if isinstance(g, int) and g == 0:
                        pe.wait_ge(bo_set, 1)
                    if live(j):
                        pe.wait_ge(at1_set, j * 2 + 2)
                    else:
                        need(pe, at_hi_set, g * 2)
                        need(pe, at_lo_set, g * 2)
                    attend(0, g, 0)
                layer1_unit(5)
                if att:
                    wo(g, 0)
                    attend(0, g, 1)

            def last_steps():
                j, m = G - 2, G - 1

                def layer1_unit(i):
                    unit(1, G, 6 + i, m, i)

                scores(1, j, 0, masked_set[0], m * 4)
                scores(1, j, 1, masked_set[0], m * 4)
                wo(m, 1)
                pe.wait_ge(x1_hi_set, m * 2 + 2)
                pe.wait_ge(x1_lo_set, m * 2 + 2)
                layer1_unit(0)
                layer1_unit(1)
                layer1_unit(2)
                pe.wait_ge(at_hi_set, G * 2)
                pe.wait_ge(at_lo_set, G * 2)
                attend(1, j, 0)
                layer1_unit(3)
                pe.wait_ge(at1_set, j * 2 + 1)
                attend(1, j, 1)
                layer1_unit(4)
                scores(1, m, 0, masked_set[1], m * 4 - 4)
                scores(1, m, 1, masked_set[1], m * 4 - 4)
                layer1_unit(5)
                for b in range(GB):
                    pe.wait_ge(at1_set, m * 2 + b)
                    attend(1, m, b)

            def bias_product():
                pe.wait_ge(bv_split, 2)
                pe.wait_ge(w_hi_set, FIRST_W + 2)
                pe.wait_ge(w_lo_set, FIRST_W + 2)
                project(ps_att, lambda c: at_hi[:, c, :], lambda c: at_lo[:, c, :], "o0", bv_wo_done)

            steps(pe, phase_a, phase_b, last_steps, bias_product)

        @block.scalar
        def _(act):
            small = [(bq_col[0], "bq0"), (bk_col[0], "bk0"), (bv0_col, "bv0"), (bq_col[1], "bq1"), (bk_col[1], "bk1")]
            for tile, n in small:
                act.dma_start(tile[:], biases[n + "_col"]).then_inc(small_in, 16)
            for tile, n in ((bo_row, "bo0"), (bv1_row, "bv1")):
                act.dma_start(tile[:], biases[n].rearrange("(a n) -> a n", a=1).to_broadcast([P, D])
                              ).then_inc(small_in, 16)
            for tile in mask:
                act.dma_start(tile[:], adj).then_inc(small_in, 16)
            halves = [(n, half) for n in WEIGHTS for half in range(2)]

            def weight_high(i):
                n, half = halves[i]
                act.wait_ge(staged[i % N_STAGE], 16 * (i // N_STAGE + 1))
                act.wait_ge(w_hi_set, i)
                act.activation(w_hi[n][:, 2 * half:2 * half + 2, :].rearrange("p c n -> p (c n)"),
                               stage[i % N_STAGE], ACT.Copy).then_inc(w_hi_set, 1)

            for i in range(DVE_W, FIRST_W):
                weight_high(i)
            act.wait_ge(small_in, 16 * 9)

            def zero_k():
                act.wait_ge(zeros_set, 1)
                for part in (k_hi, k_lo):
                    for b in range(GB):
                        act.activation(part[:, b].rearrange("p c e n -> p (c e n)"), x1[:].rearrange("p b n -> p (b n)"),
                                       ACT.Copy).then_inc(zeros_set, 1)


            def qk_out(l, u, group, i, taken_by, times, split_by, halves_split):
                act.wait_ge(qk_done[l], group * 4 + i + 1)
                if i < 2:
                    need(act, score_done[taken_by], times)
                else:
                    need(act, k_lo_even_set[split_by], halves_split)
                    need(act, k_lo_odd_set[split_by], halves_split)
                for n in range(2):
                    m = 2 * (i % 2) + n
                    src = ps_proj[u % 2][:, n * T:(n + 1) * T]
                    if i < 2:
                        dst = q_hi[:, m, :]
                    else:
                        dst = k_raw[:, n, :].rearrange("p (b j n) -> p b n j", b=GB, n=SQ)
                        src = src.rearrange("p (b n j) -> p b n j", b=GB, j=BLK)
                    bias = (bq_col if i < 2 else bk_col)[l]
                    last = act.activation(dst, src, ACT.Identity, bias=bias[:, m:m + 1])
                last.then_inc((q_hi_set if i < 2 else k_raw_set)[l], 1)

            def v_out(l, u, group, b, used_by, times):
                act.wait_ge(v_done[l], group * 2 + b + 1)
                need(act, att_done[used_by], times)
                act.activation(v[l][b][:], ps_proj[u % 2][:, :], ACT.Copy).then_inc(v_set[l], 1)

            def exps(l, group, b, i):
                act.wait_ge(masked_set[l], group * 4 + 2 * b + i + 1)
                for n in range(HB):
                    last = act.activation(prob[b][:, i, n, :], prob[b][:, i, n, :], ACT.Exp,
                                          bias=neg_max[l][b][:, i, n:n + 1], scale=-1.0,
                                          accum_out=row_sum[l][b][:, i, n:n + 1])
                last.then_inc(exp_set[l], 1)

            def x1_high(m, b):
                act.wait_ge(x1t_in[b], (m + 1) * 16 * BLK)
                need(act, qk_done[1], m * 4)
                need(act, v_done[1], m * 2)
                act.activation(x1_part(xt_hi, b), x1_turned[b].rearrange("p n c t -> p c n t"), ACT.Copy
                               ).then_inc(x1_hi_set, 1)

            def at1_copy(j, b):
                act.wait_ge(att_done[1], j * 2 + b + 1)
                act.wait_ge(blocks_set[1], j * 4 + 2 * b + 2)
                act.activation(at1[b], ps_att[:].rearrange("p (c q n) -> p c n q", c=NC, n=BLK), ACT.Copy
                               ).then_inc(at1_set, 1)

            def phase_a(g):
                j, m = g - 2, g - 1
                att, proj, xt = live(j), live(g), live(m)

                def q_or_k(i):
                    if proj:
                        l, last = (1, j) if att else (0, g - 1)
                        qk_out(0, i, g, i, l, last * 4 + 4,
                               *((0, g * 2 + 1) if i == 3 else (l, last * 2 + 2)))

                def at1_out(b):
                    if att:
                        at1_copy(j, b)

                def more_weights(i):
                    if isinstance(g, int) and g == 0:
                        weight_high(FIRST_W + 2 * i)
                        weight_high(FIRST_W + 2 * i + 1)

                if att:
                    exps(1, j, 0, 0)
                    exps(1, j, 0, 1)
                if att:
                    exps(1, j, 1, 0)
                q_or_k(0)
                if isinstance(g, int) and g == 0:
                    zero_k()
                if att:
                    exps(1, j, 1, 1)
                q_or_k(1)
                if xt:
                    x1_high(m, 0)
                more_weights(0)
                q_or_k(2)
                more_weights(1)
                at1_out(0)
                q_or_k(3)
                more_weights(2)
                more_weights(3)
                if xt:
                    x1_high(m, 1)
                if proj:
                    v_out(0, 4, g, 0, *((1, j * 2 + 1) if att else (0, g * 2 - 1)))
                    v_out(0, 5, g, 1, 0, g * 2)

            def phase_b(g):
                j, m = g - 2, g - 1
                att, proj = live(g), live(m)

                def q_or_k(i):
                    if proj:
                        l, last = (0, g) if att else (1, m - 1)
                        qk_out(1, 6 + i, m, i, l, last * 4 + 4,
                               *((1, m * 2 + 1) if i == 3 else (l, last * 2 + 2)))

                def at_high(b):
                    if att:
                        act.wait_ge(att_done[0], g * 2 + b + 1)
                        need(act, wo_done, g * 2 + b)
                        act.activation(at_hi[:].rearrange("p c n -> p (c n)"), ps_att[:], ACT.Copy
                                       ).then_inc(at_hi_set, 1)

                if live(j):
                    at1_copy(j, 1)
                if att:
                    exps(0, g, 0, 0)
                    exps(0, g, 0, 1)
                q_or_k(0)
                q_or_k(1)
                if att:
                    exps(0, g, 1, 0)
                q_or_k(2)
                if att:
                    exps(0, g, 1, 1)
                q_or_k(3)
                at_high(0)
                if proj:
                    v_out(1, 10, m, 0, *((0, g * 2 + 1) if att else (1, m * 2 - 1)))
                    v_out(1, 11, m, 1, 1, m * 2)
                at_high(1)

            def last_steps():
                j, m = G - 2, G - 1
                x1_high(m, 0)
                exps(1, j, 0, 0)
                exps(1, j, 0, 1)
                x1_high(m, 1)
                exps(1, j, 1, 0)
                qk_out(1, 6, m, 0, 1, j * 4 + 4, 1, j * 2 + 2)
                exps(1, j, 1, 1)
                qk_out(1, 7, m, 1, 1, j * 4 + 4, 1, j * 2 + 2)
                qk_out(1, 8, m, 2, 1, j * 4 + 4, 0, m * 2 + 2)
                at1_copy(j, 0)
                qk_out(1, 9, m, 3, 1, j * 4 + 4, 1, m * 2 + 1)
                at1_copy(j, 1)
                v_out(1, 10, m, 0, 1, m * 2 - 1)
                exps(1, m, 0, 0)
                exps(1, m, 0, 1)
                v_out(1, 11, m, 1, 1, m * 2)
                exps(1, m, 1, 0)
                exps(1, m, 1, 1)
                at1_copy(m, 0)
                at1_copy(m, 1)

            steps(act, phase_a, phase_b, last_steps)

        @block.vector
        def _(dve):
            halves = [(n, half) for n in WEIGHTS for half in range(2)]

            def weight_low(i):
                n, half = halves[i]
                hi = w_hi[n][:, 2 * half:2 * half + 2, :].rearrange("p c n -> p (c n)")
                if i < DVE_W:
                    dve.wait_ge(staged[i % N_STAGE], 16 * (i // N_STAGE + 1))
                    dve.tensor_copy(hi, stage[i % N_STAGE]).then_inc(w_hi_set, 1)
                dve.wait_ge(w_hi_set, i + 1)
                dve.tensor_tensor(w_lo[n][:, 2 * half:2 * half + 2, :].rearrange("p c n -> p (c n)"),
                                  stage[i % N_STAGE], hi.bitcast(F32), ALU.subtract).then_inc(w_lo_set, 1)

            def x0_high(group, half):
                need(dve, qk_done[0], group * 4)
                need(dve, v_done[0], group * 2)
                dve.wait_ge(raw_in[half], (group + 1) * 16)
                dve.tensor_copy(x0_half(xt_hi[0], half), x0_half(xt_raw, half)).then_inc(x0_hi_set, 1)

            x0_high(0, 0)
            x0_high(0, 1)
            for i in range(FIRST_W):
                weight_low(i)
            dve.wait_ge(small_in, 16 * 9)

            def constants():
                dve.tensor_scalar(mask[0][:], mask[0][:], -1.0, 1.0, ALU.mult, ALU.add).then_inc(mask_step, 1)
                dve.wait_ge(mask_step, 1)
                dve.tensor_scalar(mask[0][:], mask[0][:], MASKED / SCALE, None, ALU.mult).then_inc(mask_step, 1)
                dve.tensor_scalar(mask[1][:], mask[1][:], 0.0, MASKED / SCALE, ALU.is_equal, ALU.mult).then_inc(mask_step, 1)
                dve.wait_ge(mask_step, 3)
                dve.tensor_copy(at_hi[:], bv0_col[:].unsqueeze(2).to_broadcast([P, NC, NODES])).then_inc(bv_split, 1)
                dve.wait_ge(bv_split, 1)
                dve.tensor_tensor(at_lo[:], bv0_col[:].unsqueeze(2).to_broadcast([P, NC, NODES]),
                                  at_hi[:].bitcast(F32), ALU.subtract).then_inc(bv_split, 1)
                dve.wait_ge(zeros_set, 1 + 2 * GB)

            def mask_scores(l, group, b, halves=range(HALVES)):
                if 0 in halves:
                    if l == 0 and live(group - 2):
                        need(dve, at1_in[b], (group - 1) * 16 * BLK)
                    elif l == 1 and live(group + 1):
                        need(dve, blocks_set[0], (group + 1) * 4 + 2 * b + 2)
                    else:
                        need(dve, blocks_set[l], group * 4 + 2 * b - 2)
                        if l == 1:
                            need(dve, at1_in[b], group * 16 * BLK)
                for i in halves:
                    dve.wait_ge(score_done[l], group * 4 + 2 * b + i + 1)
                    dve.sem_inc(dve_passed, 1)
                    for n in range(HB):
                        last = dve.tensor_tensor_reduce(prob[b][:, i, n, :], ps_score[b][i][:, n, :], mask[l][:],
                                                        -SCALE, BIG, ALU.add, ALU.min,
                                                        neg_max[l][b][:, i, n:n + 1])
                    last.then_inc(masked_set[l], 1)

            def invert_sums(l, group, b):
                for i in range(HALVES):
                    dve.wait_ge(exp_set[l], group * 4 + 2 * b + i + 1)
                    dve.reciprocal(inv_sum[l][b][:, i, :], row_sum[l][b][:, i, :]).then_inc(inv_set[l], 1)

            def q_low(l, u, group, i):
                dve.wait_ge(q_hi_set[l], group * 2 + i + 1)
                for n in range(2):
                    m = 2 * i + n
                    last = dve.scalar_tensor_tensor(q_lo[:, m, :], ps_proj[u % 2][:, n * T:(n + 1) * T],
                                                    bq_col[l][:, m:m + 1], q_hi[:, m, :].bitcast(F32),
                                                    ALU.add, ALU.subtract)
                last.then_inc(q_lo_set[l], 1)

            def k_split(l, group, i):
                dve.wait_ge(k_raw_set[l], group * 2 + i + 1)
                for e in range(2):
                    hi, raw = k_block(k_hi, i, e), k_source(e)
                    dve.tensor_copy(hi, raw).then_inc(k_hi_set[l], 1)
                dve.wait_ge(k_hi_set[l], group * 4 + 2 * i + 2)
                dve.tensor_tensor(k_block(k_lo, i, 1), raw, hi.bitcast(F32), ALU.subtract).then_inc(k_lo_odd_set[l], 1)

            def statistics(l, group, b):
                done = group * 2 + b + 1
                row = (x_res if l == 0 else y)[:, b, :]
                dve.wait_ge(sum_set[l], done)
                dve.bn_stats(stats[l][:, b, :], row).then_inc(stats_set[l], 1)
                dve.wait_ge(stats_set[l], done)
                dve.sem_inc(dve_passed, 1)
                dve.bn_aggr(mean_var[l][:, b, :], stats[l][:, b, :]).then_inc(mean_set[l], 1)
                dve.wait_ge(mean_set[l], done)
                dve.tensor_scalar(var_eps[l][:, b:b + 1], mean_var[l][:, b, 1:2], EPS, None, ALU.add
                                  ).then_inc(eps_set[l], 1)

            def normalise(l, group, b):
                done = group * 2 + b + 1
                dve.wait_ge(rstd_set[l], done)
                if l == 0:
                    need(dve, x1_blocks_set, done - 2)
                    need(dve, x1_res_set, done - 2)
                src, dst = (x_res, x1) if l == 0 else (y, y)
                dve.tensor_scalar(dst[:, b, :], src[:, b, :], mean_var[l][:, b, 0:1], rstd[l][:, b:b + 1],
                                  ALU.subtract, ALU.mult).then_inc(ln_set[l], 1)

            def transpose_blocks(l, group, b, carried, times):
                need(dve, carried, times)
                if l == 1 and b == 0 and live(group + 1):
                    dve.wait_ge(x1t_in[0], (group + 2) * 16 * BLK)
                for i in range(HALVES):
                    dve.wait_ge(norm_set[l], group * 4 + 2 * b + i + 1)
                    dve.transpose(blocks_t[:, :, i].rearrange("p n h q -> p h n q"),
                                  prob[b][:, i].rearrange("p h (n k) -> p h n k", k=SQ)).then_inc(blocks_set[l], 1)

            def transpose_x1(m, b):
                if b == 0:
                    dve.wait_ge(probt_in[0], (m + 1) * 2 * 16 * BLK)
                else:
                    dve.wait_ge(x0_lo_set, m * 2 + 4 if live(m + 1) else G * 2)
                    if live(m - 2):
                        for graph in range(GB):
                            dve.wait_ge(y_out[graph], (m - 1) * 16)
                dve.wait_ge(ln_set[0], m * 2 + b + 1)
                dve.transpose(x1_blocks[b], x1[:, b, :]).then_inc(x1_blocks_set, 1)

            def x1_low(m, b):
                dve.wait_ge(x1_hi_set, m * 2 + b + 1)
                dve.tensor_tensor(x1_part(xt_lo, b), x1_turned[b].rearrange("p n c t -> p c n t"),
                                  x1_part(xt_hi, b).bitcast(F32), ALU.subtract).then_inc(x1_lo_set, 1)

            def transpose_at1(j, b):
                dve.wait_ge(at1_set, j * 2 + b + 1)
                dve.transpose(at1_blocks[b].rearrange("p (n c f) -> p c n f", n=BLK, c=NC), at1[b]
                              ).then_inc(at1_blocks_set, 1)

            def residual1(j, b):
                dve.wait_ge(at1_in[b], (j + 1) * 16 * BLK)
                dve.wait_ge(x0_lo_set, j * 2 + 6 if live(j + 2) else G * 2)
                dve.wait_ge(x1t_in[1], (j + 2 if live(j + 1) else G) * 16 * BLK)
                dve.wait_ge(x1_lo_set, j * 2 + 4 if live(j + 1) else G * 2)
                if not isinstance(j, int) or j > 0:
                    dve.wait_ge(y_out[b], j * 16)
                dve.wait_ge(x1_res_set, j * 2 + b + 1)
                total, other = (t[:, b, :].rearrange("p (c r f) -> p r c f", c=NC, r=BLK) for t in (y, x1_res))
                dve.tensor_tensor(total, at1_turned[b], other, ALU.add).then_inc(sum_set[1], 1)

            def at_low(g, b):
                dve.wait_ge(at_hi_set, g * 2 + b + 1)
                dve.tensor_tensor(at_lo[:].rearrange("p c n -> p (c n)"), ps_att[:],
                                  at_hi[:].rearrange("p c n -> p (c n)").bitcast(F32), ALU.subtract
                                  ).then_inc(at_lo_set, 1)

            def residual0(g, b):
                dve.wait_ge(wo_done, g * 2 + b + 1)
                dve.wait_ge(x_res_set, g + 1)
                dve.tensor_tensor(x_res[:, b, :], ps_proj[b][:, :], x_res[:, b, :], ALU.add).then_inc(sum_set[0], 1)

            def phase_a(g):
                j, m = g - 2, g - 1
                per = 2 * 16 * BLK

                def more_weights(i):
                    if isinstance(g, int) and g == 0:
                        weight_low(FIRST_W + 2 * i)
                        weight_low(FIRST_W + 2 * i + 1)

                if live(j):
                    mask_scores(1, j, 0, (0,))
                if live(m) and live(g):
                    x0_high(g, 1)
                if live(j):
                    mask_scores(1, j, 0, (1,))
                if live(m):
                    normalise(0, m, 0)
                    transpose_x1(m, 0)
                if live(j):
                    mask_scores(1, j, 1, (0,))
                    invert_sums(1, j, 0)
                    mask_scores(1, j, 1, (1,))
                if live(m):
                    residual0(m, 1)
                    statistics(0, m, 1)
                if live(g):
                    q_low(0, 0, g, 0)
                if live(j):
                    transpose_blocks(1, j, 0, *((probt_in[0], g * per) if live(m) else (probt_in[1], j * per)))
                if isinstance(g, int) and g == 0:
                    constants()
                if live(m):
                    normalise(0, m, 1)
                if live(g):
                    q_low(0, 1, g, 1)
                if live(m):
                    transpose_x1(m, 1)
                    x1_low(m, 0)
                more_weights(0)
                if live(j):
                    invert_sums(1, j, 1)
                if live(g):
                    k_split(0, g, 0)
                more_weights(1)
                if live(j):
                    transpose_blocks(1, j, 1, probt_in[1], j * per + per // 2)
                if live(j):
                    transpose_at1(j, 0)
                if live(g):
                    k_split(0, g, 1)
                more_weights(2)
                more_weights(3)
                if live(m):
                    x1_low(m, 1)

            def phase_b(g):
                j, m = g - 2, g - 1
                per = 2 * 16 * BLK
                att = live(g)
                if live(j):
                    transpose_at1(j, 1)
                if att:
                    mask_scores(0, g, 0)
                if live(j):
                    residual1(j, 0)
                    statistics(1, j, 0)
                if att:
                    invert_sums(0, g, 0)
                if live(m):
                    q_low(1, 6, m, 0)
                if att:
                    mask_scores(0, g, 1, (0,))
                    transpose_blocks(0, g, 0, *((probt_in[1], j * per + per) if live(j) else (probt_in[0], g * per)))
                if live(m):
                    q_low(1, 7, m, 1)
                if att:
                    mask_scores(0, g, 1, (1,))
                if live(j):
                    normalise(1, j, 0)
                if live(m):
                    k_split(1, m, 0)
                if att:
                    invert_sums(0, g, 1)
                if att:
                    transpose_blocks(0, g, 1, probt_in[0], g * per + per // 2)
                if live(j):
                    residual1(j, 1)
                    statistics(1, j, 1)
                if att:
                    at_low(g, 0)
                if live(j):
                    normalise(1, j, 1)
                if live(m):
                    k_split(1, m, 1)
                if not isinstance(g, int) or g + 1 < G:
                    x0_high(g + 1, 0)
                if att:
                    residual0(g, 0)
                    statistics(0, g, 0)
                    at_low(g, 1)

            def last_steps():
                j, m = G - 2, G - 1
                per = 2 * 16 * BLK
                mask_scores(1, j, 0)
                normalise(0, m, 0)
                transpose_x1(m, 0)
                mask_scores(1, j, 1)
                residual0(m, 1)
                statistics(0, m, 1)
                invert_sums(1, j, 0)
                normalise(0, m, 1)
                transpose_x1(m, 1)
                x1_low(m, 0)
                x1_low(m, 1)
                transpose_blocks(1, j, 0, probt_in[0], G * per)
                q_low(1, 6, m, 0)
                invert_sums(1, j, 1)
                q_low(1, 7, m, 1)
                transpose_blocks(1, j, 1, probt_in[1], j * per + per // 2)
                k_split(1, m, 0)
                transpose_at1(j, 0)
                k_split(1, m, 1)
                transpose_at1(j, 1)
                residual1(j, 0)
                statistics(1, j, 0)
                normalise(1, j, 0)
                mask_scores(1, m, 0)
                residual1(j, 1)
                statistics(1, j, 1)
                mask_scores(1, m, 1)
                invert_sums(1, m, 0)
                normalise(1, j, 1)
                transpose_blocks(1, m, 0, probt_in[1], m * per)
                invert_sums(1, m, 1)
                transpose_blocks(1, m, 1, probt_in[1], m * per + per // 2)
                transpose_at1(m, 0)
                transpose_at1(m, 1)
                for b in range(GB):
                    residual1(m, b)
                    statistics(1, m, b)
                    normalise(1, m, b)

            def add_bias_product():
                dve.wait_ge(w_lo_set, 2 * len(WEIGHTS))
                dve.wait_ge(bv_wo_done, 1)
                dve.tensor_tensor(bo_row[:], ps_att[:], bo_row[:], ALU.add).then_inc(bo_set, 1)

            for g in range(3):
                phase_a(g)
                if g == 0:
                    add_bias_product()
                phase_b(g)
            with dve.Fori(3, G - 1) as g:
                phase_a(g)
                phase_b(g)
            phase_a(G - 1)
            phase_b(G - 1)
            last_steps()

        @block.gpsimd
        def _(pool):
            pool.memset(x1[:], 0.0).then_inc(zeros_set, 1)

            def x0_low(group, half):
                pool.wait_ge(x0_hi_set, group * 2 + half + 1)
                pool.tensor_tensor(x0_half(xt_lo[0], half), x0_half(xt_raw, half), x0_half(xt_hi[0], half).bitcast(F32),
                                   ALU.subtract).then_inc(x0_lo_set, 1)

            def inverse_deviation(l, group, b):
                done = group * 2 + b + 1
                pool.wait_ge(eps_set[l], done)
                need(pool, ln_set[l], done - 2)
                pool.tensor_tensor(rstd[l][:, b:b + 1], var_eps[l][:, b:b + 1], minus_half[:], ALU.pow
                                   ).then_inc(rstd_set[l], 1)

            def normalise_probs(l, group, b):
                for i in range(HALVES):
                    pool.wait_ge(inv_set[l], group * 4 + 2 * b + i + 1)
                    pool.tensor_tensor(prob[b][:, i], prob[b][:, i],
                                       inv_sum[l][b][:, i, :].unsqueeze(2).to_broadcast([P, HB, NODES]), ALU.mult
                                       ).then_inc(norm_set[l], 1)

            def k_low_even(l, group, i):
                pool.wait_ge(k_hi_set[l], group * 4 + 2 * i + 1)
                pool.tensor_tensor(k_block(k_lo, i, 0), k_source(0), k_block(k_hi, i, 0).bitcast(F32), ALU.subtract
                                   ).then_inc(k_lo_even_set[l], 1)

            def copy_x1(m, b):
                pool.wait_ge(ln_set[0], m * 2 + b + 1)
                need(pool, sum_set[1], m * 2 + b - 1)
                pool.tensor_tensor(x1_res[:, b, :], x1[:, b, :], bv1_row[:], ALU.add).then_inc(x1_res_set, 1)

            def phase_a(g):
                j, m = g - 2, g - 1
                if live(m) and live(g):
                    x0_low(g, 1)
                if live(j):
                    normalise_probs(1, j, 0)
                if live(m):
                    inverse_deviation(0, m, 1)
                if live(j):
                    normalise_probs(1, j, 1)
                if live(g):
                    k_low_even(0, g, 0)
                    k_low_even(0, g, 1)
                    pool.wait_ge(x_in, (g + 1) * 16)
                    if isinstance(g, int) and g == 0:
                        pool.wait_ge(bo_set, 1)
                    pool.tensor_tensor(x_res[:], x_res[:], bo_row[:].unsqueeze(1).to_broadcast([P, GB, D]), ALU.add
                                       ).then_inc(x_res_set, 1)

            def phase_b(g):
                j, m = g - 2, g - 1
                if live(g):
                    normalise_probs(0, g, 0)
                if live(j):
                    inverse_deviation(1, j, 0)
                if live(m):
                    k_low_even(1, m, 0)
                if live(g):
                    normalise_probs(0, g, 1)
                if live(j):
                    inverse_deviation(1, j, 1)
                if live(m):
                    k_low_even(1, m, 1)
                    copy_x1(m, 0)
                    copy_x1(m, 1)
                if live(g):
                    if not isinstance(g, int) or g + 1 < G:
                        x0_low(g + 1, 0)
                    inverse_deviation(0, g, 0)

            def last_steps():
                j, m = G - 2, G - 1
                inverse_deviation(0, m, 1)
                normalise_probs(1, j, 0)
                normalise_probs(1, j, 1)
                k_low_even(1, m, 0)
                k_low_even(1, m, 1)
                inverse_deviation(1, j, 0)
                copy_x1(m, 0)
                inverse_deviation(1, j, 1)
                normalise_probs(1, m, 0)
                normalise_probs(1, m, 1)
                copy_x1(m, 1)
                inverse_deviation(1, m, 0)
                inverse_deviation(1, m, 1)

            pool.memset(minus_half[:], -0.5).then_inc(consts_set, 1)
            pool.wait_ge(consts_set, 1)
            x0_low(0, 0)
            x0_low(0, 1)
            for g in range(3):
                phase_a(g)
                phase_b(g)
            with pool.Fori(3, G - 1) as g:
                phase_a(g)
                phase_b(g)
            phase_a(G - 1)
            phase_b(G - 1)
            last_steps()


def kernel(**inputs):
    import numpy as np
    import concourse.bacc as bacc
    from concourse.bass_utils import run_bass_kernel_spmd

    nc = bacc.Bacc("TRN2", target_bir_lowering=False, num_devices=1)
    x = np.asarray(inputs["x"])
    graphs = x.shape[0]
    groups = graphs // GB
    arrays = {
        "x_tok": np.ascontiguousarray(x.reshape(groups, GB, NODES, D).transpose(0, 2, 1, 3)),
        "x_feat": np.ascontiguousarray(x.reshape(groups, T, NC, P).transpose(0, 3, 2, 1)),
        "adj": np.ascontiguousarray(
            np.asarray(inputs["adj"]).reshape(NODES, SQ, BLK).transpose(0, 2, 1).reshape(NODES, NODES)),
    }
    names = {"q0": "L0_gnn_Wq", "k0": "L0_gnn_Wk", "v0": "L0_gnn_Wv", "o0": "L0_gnn_Wo",
             "q1": "L1_gnn_Wq", "k1": "L1_gnn_Wk", "v1": "L1_gnn_Wv"}
    for short, name in names.items():
        w = np.asarray(inputs[name])
        if short in ("q1", "k1", "v1"):
            w = w.reshape(BLK, NC, SQ, D).transpose(1, 2, 0, 3).reshape(D, D)
        arrays[f"w_{short}"] = np.ascontiguousarray(w)
        bias = np.asarray(inputs[name.replace("_W", "_b")])
        arrays[f"b_{short}"] = np.ascontiguousarray(bias)
        arrays[f"b_{short}_col"] = np.ascontiguousarray(bias.reshape(NC, P).T)
    aps = {n: nc.dram_tensor(n, a.shape, mybir.dt.from_np(a.dtype), kind="ExternalInput").ap()
           for n, a in arrays.items()}
    out = nc.dram_tensor("out", (groups, GB, NODES, D), F32, kind="ExternalOutput").ap()
    adj_resnorm_kernel(nc, aps["x_tok"], aps["x_feat"], aps["adj"], {s: aps[f"w_{s}"] for s in names},
                       {n.replace("b_", "b"): ap for n, ap in aps.items() if n.startswith("b_")}, out)
    result = run_bass_kernel_spmd(nc, [arrays], core_ids=[0])
    return result.results[0]["out"].reshape(graphs, NODES, D)
```
